# Optimizing a Trainium2 kernel written in Bass

```python
import numpy as np
import jax
import jax.numpy as jnp

def _softmax(x, axis=-1):
    return jax.nn.softmax(x, axis=axis)

def _gelu(x):
    return jax.nn.gelu(x, approximate=True)

def _silu(x):
    return jax.nn.silu(x)

def _sigmoid(x):
    return jax.nn.sigmoid(x)

def _layernorm(x, axis=-1, eps=1e-05):
    m = jnp.mean(x, axis=axis, keepdims=True)
    v = jnp.var(x, axis=axis, keepdims=True)
    return (x - m) / jnp.sqrt(v + eps)

def _scatter_add(tgt, idx, src, axis=0):
    return tgt.at[idx].add(src)

def _segment_sum(src, seg, n):
    return jax.ops.segment_sum(src, seg, n)
kernel_name = 'mk_dlrm_tower_d1_rec_r8_59ae17'

def setup_inputs(seed: int=0):
    np.random.seed(seed)
    _w = jnp.asarray

    def _rec_inputs():
        import jax
        import jax.numpy as jnp
        _tk = jax.random.key(seed)
        dense_ctx = jax.random.normal(jax.random.fold_in(_tk, 190), (1024, 16), jnp.float32)
        ids = jnp.stack([jax.random.randint(jax.random.fold_in(_tk, 200 + f), (1024,), 0, v, jnp.int32) for f, v in enumerate([125000, 1250, 12500, 12500, 1250, 1250, 1000, 1250, 1250, 1000, 12500, 12500, 125000, 12500, 12500, 1000, 1000, 1000, 1250, 1000, 125000, 12500, 12500, 125000, 125000, 125000, 1000, 1000, 125000, 125000, 1250, 1250, 125000, 12500, 125000, 1000, 1000, 125000, 125000])], axis=1)
        tbl_0 = 0.05 * jax.random.normal(jax.random.fold_in(_tk, 500 + 0), (125000, 16), jnp.float32)
        tbl_1 = 0.05 * jax.random.normal(jax.random.fold_in(_tk, 500 + 1), (1250, 16), jnp.float32)
        tbl_2 = 0.05 * jax.random.normal(jax.random.fold_in(_tk, 500 + 2), (12500, 16), jnp.float32)
        tbl_3 = 0.05 * jax.random.normal(jax.random.fold_in(_tk, 500 + 3), (12500, 16), jnp.float32)
        tbl_4 = 0.05 * jax.random.normal(jax.random.fold_in(_tk, 500 + 4), (1250, 16), jnp.float32)
        tbl_5 = 0.05 * jax.random.normal(jax.random.fold_in(_tk, 500 + 5), (1250, 16), jnp.float32)
        tbl_6 = 0.05 * jax.random.normal(jax.random.fold_in(_tk, 500 + 6), (1000, 16), jnp.float32)
        tbl_7 = 0.05 * jax.random.normal(jax.random.fold_in(_tk, 500 + 7), (1250, 16), jnp.float32)
        tbl_8 = 0.05 * jax.random.normal(jax.random.fold_in(_tk, 500 + 8), (1250, 16), jnp.float32)
        tbl_9 = 0.05 * jax.random.normal(jax.random.fold_in(_tk, 500 + 9), (1000, 16), jnp.float32)
        tbl_10 = 0.05 * jax.random.normal(jax.random.fold_in(_tk, 500 + 10), (12500, 16), jnp.float32)
        tbl_11 = 0.05 * jax.random.normal(jax.random.fold_in(_tk, 500 + 11), (12500, 16), jnp.float32)
        tbl_12 = 0.05 * jax.random.normal(jax.random.fold_in(_tk, 500 + 12), (125000, 16), jnp.float32)
        tbl_13 = 0.05 * jax.random.normal(jax.random.fold_in(_tk, 500 + 13), (12500, 16), jnp.float32)
        tbl_14 = 0.05 * jax.random.normal(jax.random.fold_in(_tk, 500 + 14), (12500, 16), jnp.float32)
        tbl_15 = 0.05 * jax.random.normal(jax.random.fold_in(_tk, 500 + 15), (1000, 16), jnp.float32)
        tbl_16 = 0.05 * jax.random.normal(jax.random.fold_in(_tk, 500 + 16), (1000, 16), jnp.float32)
        tbl_17 = 0.05 * jax.random.normal(jax.random.fold_in(_tk, 500 + 17), (1000, 16), jnp.float32)
        tbl_18 = 0.05 * jax.random.normal(jax.random.fold_in(_tk, 500 + 18), (1250, 16), jnp.float32)
        tbl_19 = 0.05 * jax.random.normal(jax.random.fold_in(_tk, 500 + 19), (1000, 16), jnp.float32)
        tbl_20 = 0.05 * jax.random.normal(jax.random.fold_in(_tk, 500 + 20), (125000, 16), jnp.float32)
        tbl_21 = 0.05 * jax.random.normal(jax.random.fold_in(_tk, 500 + 21), (12500, 16), jnp.float32)
        tbl_22 = 0.05 * jax.random.normal(jax.random.fold_in(_tk, 500 + 22), (12500, 16), jnp.float32)
        tbl_23 = 0.05 * jax.random.normal(jax.random.fold_in(_tk, 500 + 23), (125000, 16), jnp.float32)
        tbl_24 = 0.05 * jax.random.normal(jax.random.fold_in(_tk, 500 + 24), (125000, 16), jnp.float32)
        tbl_25 = 0.05 * jax.random.normal(jax.random.fold_in(_tk, 500 + 25), (125000, 16), jnp.float32)
        tbl_26 = 0.05 * jax.random.normal(jax.random.fold_in(_tk, 500 + 26), (1000, 16), jnp.float32)
        tbl_27 = 0.05 * jax.random.normal(jax.random.fold_in(_tk, 500 + 27), (1000, 16), jnp.float32)
        tbl_28 = 0.05 * jax.random.normal(jax.random.fold_in(_tk, 500 + 28), (125000, 16), jnp.float32)
        tbl_29 = 0.05 * jax.random.normal(jax.random.fold_in(_tk, 500 + 29), (125000, 16), jnp.float32)
        tbl_30 = 0.05 * jax.random.normal(jax.random.fold_in(_tk, 500 + 30), (1250, 16), jnp.float32)
        tbl_31 = 0.05 * jax.random.normal(jax.random.fold_in(_tk, 500 + 31), (1250, 16), jnp.float32)
        tbl_32 = 0.05 * jax.random.normal(jax.random.fold_in(_tk, 500 + 32), (125000, 16), jnp.float32)
        tbl_33 = 0.05 * jax.random.normal(jax.random.fold_in(_tk, 500 + 33), (12500, 16), jnp.float32)
        tbl_34 = 0.05 * jax.random.normal(jax.random.fold_in(_tk, 500 + 34), (125000, 16), jnp.float32)
        tbl_35 = 0.05 * jax.random.normal(jax.random.fold_in(_tk, 500 + 35), (1000, 16), jnp.float32)
        tbl_36 = 0.05 * jax.random.normal(jax.random.fold_in(_tk, 500 + 36), (1000, 16), jnp.float32)
        tbl_37 = 0.05 * jax.random.normal(jax.random.fold_in(_tk, 500 + 37), (125000, 16), jnp.float32)
        tbl_38 = 0.05 * jax.random.normal(jax.random.fold_in(_tk, 500 + 38), (125000, 16), jnp.float32)
        _rk = jax.random.fold_in(_tk, 7)
        W_top1 = 0.0606339 * jax.random.normal(jax.random.fold_in(_tk, 801), (272, 512), jnp.float32)
        W_top2 = 0.0441942 * jax.random.normal(jax.random.fold_in(_tk, 802), (512, 256), jnp.float32)
        W_top3 = 0.0625 * jax.random.normal(jax.random.fold_in(_tk, 803), (256, 1), jnp.float32)
        b_top1 = jnp.zeros((512,), jnp.float32)
        b_top2 = jnp.zeros((256,), jnp.float32)
        return (dense_ctx, ids, tbl_0, tbl_1, tbl_2, tbl_3, tbl_4, tbl_5, tbl_6, tbl_7, tbl_8, tbl_9, tbl_10, tbl_11, tbl_12, tbl_13, tbl_14, tbl_15, tbl_16, tbl_17, tbl_18, tbl_19, tbl_20, tbl_21, tbl_22, tbl_23, tbl_24, tbl_25, tbl_26, tbl_27, tbl_28, tbl_29, tbl_30, tbl_31, tbl_32, tbl_33, tbl_34, tbl_35, tbl_36, tbl_37, tbl_38, W_top1, b_top1, W_top2, b_top2, W_top3)
    dense_ctx, ids, tbl_0, tbl_1, tbl_2, tbl_3, tbl_4, tbl_5, tbl_6, tbl_7, tbl_8, tbl_9, tbl_10, tbl_11, tbl_12, tbl_13, tbl_14, tbl_15, tbl_16, tbl_17, tbl_18, tbl_19, tbl_20, tbl_21, tbl_22, tbl_23, tbl_24, tbl_25, tbl_26, tbl_27, tbl_28, tbl_29, tbl_30, tbl_31, tbl_32, tbl_33, tbl_34, tbl_35, tbl_36, tbl_37, tbl_38, W_top1, b_top1, W_top2, b_top2, W_top3 = _rec_inputs()

    def _L0_rec_setup():
        import jax, jax.numpy as jnp
        import numpy as np
        B, F0, D = (256, 39, 16)
        H1, H2 = (128, 128)
        key = jax.random.key(seed)
        k1, k2, k3 = jax.random.split(key, 3)
        x = jax.random.normal(k1, (B, F0, D), dtype=jnp.float32)

        def xavier(k, out_c, in_c):
            bound = np.sqrt(6.0 / (in_c + out_c)).astype(np.float32)
            return jax.random.uniform(k, (out_c, in_c, 1), dtype=jnp.float32, minval=-bound, maxval=bound)
        W0 = xavier(k2, H1, F0 * F0)
        W1 = xavier(k3, H2, F0 * H1)
        return {'input': x, 'W0': W0, 'W1': W1}
    _L0_rec_all = _L0_rec_setup()
    _L0_rec_in = {k: v for k, v in _L0_rec_all.items() if k in ('W0', 'W1')}
    del _L0_rec_all
    return {'dense_ctx': dense_ctx, 'ids': ids, 'tbl_0': tbl_0, 'tbl_1': tbl_1, 'tbl_2': tbl_2, 'tbl_3': tbl_3, 'tbl_4': tbl_4, 'tbl_5': tbl_5, 'tbl_6': tbl_6, 'tbl_7': tbl_7, 'tbl_8': tbl_8, 'tbl_9': tbl_9, 'tbl_10': tbl_10, 'tbl_11': tbl_11, 'tbl_12': tbl_12, 'tbl_13': tbl_13, 'tbl_14': tbl_14, 'tbl_15': tbl_15, 'tbl_16': tbl_16, 'tbl_17': tbl_17, 'tbl_18': tbl_18, 'tbl_19': tbl_19, 'tbl_20': tbl_20, 'tbl_21': tbl_21, 'tbl_22': tbl_22, 'tbl_23': tbl_23, 'tbl_24': tbl_24, 'tbl_25': tbl_25, 'tbl_26': tbl_26, 'tbl_27': tbl_27, 'tbl_28': tbl_28, 'tbl_29': tbl_29, 'tbl_30': tbl_30, 'tbl_31': tbl_31, 'tbl_32': tbl_32, 'tbl_33': tbl_33, 'tbl_34': tbl_34, 'tbl_35': tbl_35, 'tbl_36': tbl_36, 'tbl_37': tbl_37, 'tbl_38': tbl_38, 'W_top1': W_top1, 'b_top1': b_top1, 'W_top2': W_top2, 'b_top2': b_top2, 'W_top3': W_top3, 'L0_rec_W0': _L0_rec_in['W0'], 'L0_rec_W1': _L0_rec_in['W1']}

def reference(dense_ctx, ids, tbl_0, tbl_1, tbl_2, tbl_3, tbl_4, tbl_5, tbl_6, tbl_7, tbl_8, tbl_9, tbl_10, tbl_11, tbl_12, tbl_13, tbl_14, tbl_15, tbl_16, tbl_17, tbl_18, tbl_19, tbl_20, tbl_21, tbl_22, tbl_23, tbl_24, tbl_25, tbl_26, tbl_27, tbl_28, tbl_29, tbl_30, tbl_31, tbl_32, tbl_33, tbl_34, tbl_35, tbl_36, tbl_37, tbl_38, W_top1, b_top1, W_top2, b_top2, W_top3, L0_rec_W0, L0_rec_W1):
    import jax
    import jax.numpy as jnp

    def _L0_rec_ref(input, W0, W1):
        import jax, jax.numpy as jnp
        import numpy as np
        B, F0, D = (256, 39, 16)
        H1, H2 = (128, 128)
        x0 = input
        h = input
        outs = []
        for W in (W0, W1):
            Hout, P, _ = W.shape
            Hk = h.shape[1]
            Wr = W[:, :, 0].reshape(Hout, x0.shape[1], Hk)
            h = jnp.einsum('bfd,bqd,hfq->bhd', x0, h, Wr)
            outs.append(h)
        result = jnp.concatenate(outs, axis=1)
        return jnp.sum(result, axis=2)
    e = jnp.stack([tbl_0[ids[:, 0]], tbl_1[ids[:, 1]], tbl_2[ids[:, 2]], tbl_3[ids[:, 3]], tbl_4[ids[:, 4]], tbl_5[ids[:, 5]], tbl_6[ids[:, 6]], tbl_7[ids[:, 7]], tbl_8[ids[:, 8]], tbl_9[ids[:, 9]], tbl_10[ids[:, 10]], tbl_11[ids[:, 11]], tbl_12[ids[:, 12]], tbl_13[ids[:, 13]], tbl_14[ids[:, 14]], tbl_15[ids[:, 15]], tbl_16[ids[:, 16]], tbl_17[ids[:, 17]], tbl_18[ids[:, 18]], tbl_19[ids[:, 19]], tbl_20[ids[:, 20]], tbl_21[ids[:, 21]], tbl_22[ids[:, 22]], tbl_23[ids[:, 23]], tbl_24[ids[:, 24]], tbl_25[ids[:, 25]], tbl_26[ids[:, 26]], tbl_27[ids[:, 27]], tbl_28[ids[:, 28]], tbl_29[ids[:, 29]], tbl_30[ids[:, 30]], tbl_31[ids[:, 31]], tbl_32[ids[:, 32]], tbl_33[ids[:, 33]], tbl_34[ids[:, 34]], tbl_35[ids[:, 35]], tbl_36[ids[:, 36]], tbl_37[ids[:, 37]], tbl_38[ids[:, 38]]], axis=1)
    z = _L0_rec_ref(e, L0_rec_W0, L0_rec_W1)
    z = z.reshape(z.shape[0], -1)
    h = jnp.concatenate([z, dense_ctx], axis=1)
    h = jnp.maximum(h @ W_top1 + b_top1, 0.0)
    h = jnp.maximum(h @ W_top2 + b_top2, 0.0)
    y = h @ W_top3
    return y

_drawn_inputs = setup_inputs


def setup_inputs(seed=0):
    import zlib

    import numpy as np

    out = dict(_drawn_inputs(seed))
    spreads = {'b_top1': (0.0, 0.1), 'b_top2': (0.0, 0.1)}
    factors = {'tbl_0': 6.76,
     'tbl_1': 6.685,
     'tbl_2': 6.597,
     'tbl_3': 7.222,
     'tbl_4': 7.061,
     'tbl_5': 7.206,
     'tbl_6': 7.018,
     'tbl_7': 7.301,
     'tbl_8': 7.36,
     'tbl_9': 7.455,
     'tbl_10': 6.74,
     'tbl_11': 6.937,
     'tbl_12': 7.509,
     'tbl_13': 7.471,
     'tbl_14': 7.186,
     'tbl_15': 7.141,
     'tbl_16': 7.008,
     'tbl_17': 7.577,
     'tbl_18': 7.378,
     'tbl_19': 7.272,
     'tbl_20': 6.793,
     'tbl_21': 7.583,
     'tbl_22': 7.621,
     'tbl_23': 7.426,
     'tbl_24': 6.308,
     'tbl_25': 7.198,
     'tbl_26': 6.678,
     'tbl_27': 6.973,
     'tbl_28': 7.316,
     'tbl_29': 7.156,
     'tbl_30': 6.748,
     'tbl_31': 7.014,
     'tbl_32': 6.836,
     'tbl_33': 7.409,
     'tbl_34': 6.833,
     'tbl_35': 7.001,
     'tbl_36': 7.367,
     'tbl_37': 6.524,
     'tbl_38': 7.058,
     'L0_rec_W1': 8.0}
    for name, (base, spread) in spreads.items():
        noise = np.random.default_rng([zlib.crc32(name.encode()), seed]).standard_normal(out[name].shape)
        drawn = base * np.exp(spread * noise) if base else spread * noise
        out[name] = jnp.asarray(drawn.astype(out[name].dtype))
    for name, factor in factors.items():
        out[name] = (out[name] * factor).astype(out[name].dtype)
    return out
```

```python
import numpy as np
import concourse.bass as bass
from concourse import mybir
from contextlib import ExitStack

BATCH = 1024
F = 39
D = 16
H = 128
CTX = 16
M1, M2 = 512, 256

BT = 128
TILES = BATCH // BT
CB = 32
CHUNKS = BT // CB
COLS = CB * D
GROUPS = 4
GB = CB // GROUPS
FO = F + 1

SHIFTS = ((0, 1, 6, 31), (0, 2, 12, 23), (0, 3, 7, 22))
LAST_SHIFTS = (0, 13)
SOURCES = 5
PAIRS = ((0, 1), (0, 2), (1, 2), (0, 3), (1, 3), (2, 3), (0, 4))
NP = len(PAIRS)
KEPT = 3
USED_UP = tuple(max([k + 1 for k, p in enumerate(PAIRS) if p[1] == j], default=0) for j in range(SOURCES))
PARTS = 3
HALF = (0, 20, F)


def fields_of(source):
    shifts = LAST_SHIFTS if source == 4 else [s[source] for s in SHIFTS]
    return [(F * g + p, (p + s) % F) for g, s in enumerate(shifts) for p in range(F)]


def build(nc, ids, tables, ctx_t, w0_ab, w0_ba, w1, select, select_t, own, ident, w_top1z, w_top1c,
          b_top1, w_top2, b_top2, w_top3, out):
    f32, bf16, i32 = mybir.dt.float32, mybir.dt.bfloat16, mybir.dt.int32
    ALU, ACT = mybir.AluOpType, mybir.ActivationFunctionType

    with ExitStack() as stack:
        def sb(name, shape, dt=f32):
            return stack.enter_context(nc.sbuf_tensor(name, shape, dt))

        def ps(name, shape, dt=f32):
            return stack.enter_context(nc.psum_tensor(name, shape, dt))

        def sem(name):
            return stack.enter_context(nc.semaphore(name))

        w0ab_sb = sb("w0ab_sb", [128, NP, H])
        w0ba_sb = sb("w0ba_sb", [128, NP, H])
        w0_sb = sb("w0_sb", [128, NP, H])
        w1_sb = sb("w1_sb", [H, F, H])
        select_sb = sb("select_sb", [PARTS * F, SOURCES, 128], bf16)
        select_t_sb = sb("select_t_sb", [PARTS * F, F], bf16)
        select_f = sb("select_f", [PARTS * F, SOURCES, 128])
        select_t_f = sb("select_t_f", [PARTS * F, F])
        own_sb = sb("own_sb", [128, GB])
        ident_sb = sb("ident_sb", [128, 128])
        ident_bf = sb("ident_bf", [128, 128], bf16)
        wt1z_sb = sb("wt1z_sb", [128, 2, M1])
        wt1c_sb = sb("wt1c_sb", [CTX, M1])
        bt1_sb = sb("bt1_sb", [128, M1 // 128])
        wt2_sb = sb("wt2_sb", [128, M1 // 128, M2])
        bt2_sb = sb("bt2_sb", [128, M2 // 128])
        wt3_sb = sb("wt3_sb", [128, M2 // 128])
        ids_sb = [sb(f"ids_sb{h}", [BT, HALF[h + 1] - HALF[h]], i32) for h in range(2)]
        rows_sb = [sb(f"rows_sb{h}", [BT, HALF[h + 1] - HALF[h], D]) for h in range(2)]
        rest_sb = [sb(f"rest_sb{h}", [BT, HALF[h + 1] - HALF[h], D]) for h in range(2)]
        parts_sb = sb("parts_sb", [BT, D, PARTS * F], bf16)
        parts_t = sb("parts_t", [PARTS * F, BT, D], bf16)
        kept = sb("kept", [128, 2, KEPT, COLS])
        prods = sb("prods", [128, 2, NP, COLS])
        h1_sb = sb("h1_sb", [H, 2, COLS])
        h1t_sb = sb("h1t_sb", [128, 2, GROUPS, H])
        spread = sb("spread", [128, 2, GROUPS, GB, FO])
        gram = sb("gram", [H, FO, BT])
        z_sb = sb("z_sb", [128, 2, BT])
        ctx_sb = sb("ctx_sb", [CTX, BATCH])
        m1_sb = sb("m1_sb", [128, M1 // 128, BT])
        m2_sb = sb("m2_sb", [128, M2 // 128, BT])
        y_sb = sb("y_sb", [1, BATCH])

        source_ps = [ps(f"source_ps{i}", [128, COLS]) for i in range(2)]
        h1_ps = ps("h1_ps", [H, COLS])
        h1t_ps = ps("h1t_ps", [128, GROUPS, H])
        gram_ps = ps("gram_ps", [H, 2, 512])
        x_ps = ps("x_ps", [128, 512])
        top_ps = ps("top_ps", [128, 512])
        x_bf = x_ps[0:PARTS * F, :].bitcast(bf16)

        ids_loaded = [sem(f"ids_loaded{h}") for h in range(2)]
        gathered = [sem(f"gathered{h}") for h in range(2)]
        front_loaded = sem("front_loaded")
        w0_loaded = sem("w0_loaded")
        w1_loaded = sem("w1_loaded")
        top_loaded = sem("top_loaded")
        y_stored = sem("y_stored")
        gathering = sem("gathering")
        w0_added = sem("w0_added")
        constants_set = sem("constants_set")
        first_part = [sem(f"first_part{h}") for h in range(2)]
        first_rest = [sem(f"first_rest{h}") for h in range(2)]
        second_part = [sem(f"second_part{h}") for h in range(2)]
        parts_done = [sem(f"parts_done{h}") for h in range(2)]
        turned = sem("turned")
        turned_copied = sem("turned_copied")
        selected = sem("selected")
        source_kept = sem("source_kept")
        multiplied = sem("multiplied")
        h1_ready = sem("h1_ready")
        h1_copied = sem("h1_copied")
        h1_turned = sem("h1_turned")
        h1t_copied = sem("h1t_copied")
        x_turned = sem("x_turned")
        x_spread = sem("x_spread")
        gram_ready = sem("gram_ready")
        gram_copied = sem("gram_copied")
        z2_ready = sem("z2_ready")
        z_copied = sem("z_copied")
        m1_ready = sem("m1_ready")
        m1_copied = sem("m1_copied")
        m2_ready = sem("m2_ready")
        m2_copied = sem("m2_copied")
        y_ready = sem("y_ready")
        top_free = sem("top_free")

        block = stack.enter_context(nc.Block())

        def over_tiles(eng, body):
            body(0, True, False)
            with eng.Fori(1, TILES - 1) as t:
                body(t, False, False)
            body(TILES - 1, False, True)

        @block.sync
        def _(sp):
            def load_ids(t, first):
                for h in range(2):
                    if not first:
                        sp.wait_ge(gathered[h], 16 * (HALF[h + 1] - HALF[h]) * t)
                    rows = ids.rearrange("(t p) f -> t p f", p=BT)[bass.ds(t, 1), :, HALF[h]:HALF[h + 1]]
                    sp.dma_start(ids_sb[h][:, :], rows.rearrange("t p f -> p (t f)"))\
                      .then_inc(ids_loaded[h], 16)

            load_ids(0, True)
            for to, of in ((select_f, select), (select_t_f, select_t), (own_sb, own)):
                sp.dma_start(to[:], of).then_inc(front_loaded, 16)
            sp.dma_start(w0ab_sb[:], w0_ab).then_inc(w0_loaded, 16)
            sp.dma_start(w0ba_sb[:], w0_ba).then_inc(w0_loaded, 16)
            sp.dma_start(w1_sb[:], w1).then_inc(w1_loaded, 16)
            for to, of in ((wt1z_sb, w_top1z), (wt1c_sb, w_top1c), (bt1_sb, b_top1), (wt2_sb, w_top2),
                           (bt2_sb, b_top2), (wt3_sb, w_top3), (ctx_sb, ctx_t)):
                sp.dma_start(to[:], of).then_inc(top_loaded, 16)

            with sp.Fori(1, TILES) as t:
                load_ids(t, False)
            sp.wait_ge(top_free, 1 + TILES)
            sp.dma_start(out.rearrange("(a b) o -> a (b o)", a=1), y_sb[:, :]).then_inc(y_stored, 16)
            sp.wait_ge(y_stored, 16)

        @block.gpsimd
        def _(pool):
            def gather(t, first):
                for h in range(2):
                    pool.wait_ge(ids_loaded[h], 16 * (t + 1))
                    if not first:
                        pool.wait_ge(first_rest[h], t)
                    pool.sem_inc(gathering, 1)
                    for f in range(HALF[h], HALF[h + 1]):
                        n = f - HALF[h]
                        pool.indirect_dma_start(
                            rows_sb[h][:, n, :], None, tables[f],
                            bass.IndirectOffsetOnAxis(ap=ids_sb[h][:, n:n + 1], axis=0),
                        ).then_inc(gathered[h], 16)

            gather(0, True)
            with pool.Fori(1, TILES) as t:
                gather(t, False)

        def part(which, h):
            lo = which * F
            return parts_sb[:, :, lo + HALF[h]:lo + HALF[h + 1]].rearrange("p d f -> p f d")

        @block.scalar
        def _(act):
            act.dma_start(ident_sb[:, :], ident).then_inc(front_loaded, 16)
            act.wait_ge(front_loaded, 64)
            for to, of in ((ident_bf, ident_sb), (select_sb, select_f), (select_t_sb, select_t_f)):
                act.activation(to[:], of[:], ACT.Copy).then_inc(constants_set, 1)

            def split(t, h, first):
                act.wait_ge(gathered[h], 16 * (HALF[h + 1] - HALF[h]) * (t + 1))
                if not first:
                    act.wait_ge(turned, 2 * t)
                act.activation(part(0, h), rows_sb[h][:, :, :], ACT.Copy).then_inc(first_part[h], 1)
                act.wait_ge(first_rest[h], t + 1)
                act.activation(part(1, h), rest_sb[h][:, :, :], ACT.Copy).then_inc(second_part[h], 1)

            def copy_turned(t):
                for r in range(2):
                    act.wait_ge(turned, 2 * t + r + 1)
                    act.activation(parts_t[:, :, 8 * r:8 * r + 8],
                                   x_bf.rearrange("p (d b) -> p b d", d=8), ACT.Copy)\
                       .then_inc(turned_copied, 1)

            def keep(n, c, j, first):
                act.wait_ge(selected, SOURCES * n + j + 1)
                if j == 0 and not first:
                    act.wait_ge(multiplied, NP * (n - 1))
                act.activation(kept[:, c % 2, j, :], source_ps[(SOURCES * c + j) % 2][:, :], ACT.Copy)\
                   .then_inc(source_kept, 1)

            def copy_h1(n, c, first):
                act.wait_ge(h1_ready, n + 1)
                if not first:
                    act.wait_ge(h1_turned, n - 1)
                act.activation(h1_sb[:, c % 2, :], h1_ps[:, :], ACT.Copy).then_inc(h1_copied, 1)

            def copy_gram(n, c, pair, t):
                act.wait_ge(gram_ready, 2 * n + pair + 1)
                if c == 0 and pair == 0 and not (isinstance(t, int) and t == 0):
                    act.wait_ge(z_copied, 2 * t)
                at = CB * c + 2 * GB * pair
                for g in range(2):
                    last = act.activation(
                        gram[:, :, at + GB * g:at + GB * (g + 1)],
                        gram_ps[:, g, 0:GB * FO].rearrange("p (b f) -> p f b", f=FO), ACT.Copy)
                last.then_inc(gram_copied, 1)

            def tile(t, first, last):
                for c in range(CHUNKS):
                    n = CHUNKS * t + c
                    before, after = (c - 1) % CHUNKS, (c + 1) % CHUNKS
                    has_before, has_after = not (first and c == 0), not (last and c == CHUNKS - 1)
                    t_before = t - 1 if c == 0 else t
                    if c == CHUNKS - 1 and not last:
                        copy_turned(t + 1)
                    if has_after:
                        keep(n + 1, after, 0, first and c == 0)
                        keep(n + 1, after, 1, False)
                    if has_before:
                        copy_gram(n - 1, before, 0, t_before)
                    if has_after:
                        keep(n + 1, after, 2, False)
                    copy_h1(n, c, first and c < 2)
                    if has_before:
                        copy_gram(n - 1, before, 1, t_before)
                    if c in (0, 2) and not last:
                        split(t + 1, c // 2, False)
                if last:
                    copy_gram(n, c, 0, t)
                    copy_gram(n, c, 1, t)

            split(0, 0, True)
            split(0, 1, True)
            copy_turned(0)
            for j in range(KEPT):
                keep(0, 0, j, True)
            over_tiles(act, tile)

        @block.vector
        def _(dve):
            def split(t, h):
                dve.wait_ge(first_part[h], t + 1)
                dve.tensor_tensor(rest_sb[h][:, :, :], rows_sb[h][:, :, :], part(0, h), ALU.subtract)\
                   .then_inc(first_rest[h], 1)
                dve.wait_ge(second_part[h], t + 1)
                dve.tensor_tensor(part(2, h), rest_sb[h][:, :, :], part(1, h), ALU.subtract)\
                   .then_inc(parts_done[h], 1)

            def multiply(n, c, first):
                for k, (i, j) in enumerate(PAIRS):
                    if k == 0 and not first:
                        dve.wait_ge(h1_ready, n - 1)
                    dve.wait_ge(selected, SOURCES * n + j + 1)
                    dve.wait_ge(source_kept, KEPT * n + (j if j < KEPT else i) + 1)
                    dve.tensor_tensor(prods[:, c % 2, k, :], source_ps[(SOURCES * c + j) % 2][:, :],
                                      kept[:, c % 2, i, :], ALU.mult).then_inc(multiplied, 1)

            def spread_x(n, c, first):
                dve.wait_ge(x_turned, n + 1)
                if not first:
                    dve.wait_ge(gram_ready, 2 * (n - 1))
                x = x_ps[:, 0:GROUPS * F].rearrange("p (g o f) -> p g o f", g=GROUPS, o=1)
                mask = own_sb[:, :].rearrange("p (g b f) -> p g b f", g=1, f=1)
                dve.tensor_tensor(spread[:, c % 2, :, :, 0:F],
                                  x.to_broadcast([128, GROUPS, GB, F]),
                                  mask.to_broadcast([128, GROUPS, GB, F]), ALU.mult).then_inc(x_spread, 1)

            def copy_h1t(n, c, first):
                dve.wait_ge(h1_turned, n + 1)
                if not first:
                    dve.wait_ge(gram_ready, 2 * (n - 1))
                dve.tensor_copy(h1t_sb[:, c % 2, :, :], h1t_ps[:, :, :]).then_inc(h1t_copied, 1)

            def copy_z(t):
                dve.wait_ge(z2_ready, t + 1)
                dve.tensor_copy(z_sb[:, 1, :], top_ps[:, 0:BT]).then_inc(z_copied, 1)
                dve.wait_ge(gram_copied, 2 * CHUNKS * (t + 1))
                dve.tensor_copy(z_sb[:, 0, :], gram[:, F, :]).then_inc(z_copied, 1)

            def relu(ready, copied, to, bias, t):
                dve.wait_ge(ready, t + 1)
                for m in range(to.shape[1]):
                    dve.tensor_scalar(to[:, m, :], top_ps[:, m * BT:(m + 1) * BT], bias[:, m:m + 1], 0.0,
                                      ALU.add, ALU.max).then_inc(copied, 1)

            def copy_y(t):
                dve.wait_ge(y_ready, t + 1)
                dve.tensor_copy(y_sb[:, bass.ds(t * BT, BT)], top_ps[0:1, 0:BT]).then_inc(top_free, 1)

            def tile(t, first, last):
                for c in range(CHUNKS):
                    n = CHUNKS * t + c
                    if not first:
                        if c == 1:
                            copy_z(t - 1)
                        elif c == 2:
                            relu(m1_ready, m1_copied, m1_sb, bt1_sb, t - 1)
                        elif c == 3:
                            relu(m2_ready, m2_copied, m2_sb, bt2_sb, t - 1)
                    if not (first and c == 0):
                        copy_h1t(n - 1, (c - 1) % CHUNKS, first and c < 3)
                    if not (last and c == CHUNKS - 1):
                        multiply(n + 1, (c + 1) % CHUNKS, first and c == 0)
                        spread_x(n + 1, (c + 1) % CHUNKS, first and c == 0)
                    if c in (0, 2) and not last:
                        split(t + 1, c // 2)
                    if c == 3 and not first:
                        copy_y(t - 1)
                if last:
                    copy_h1t(CHUNKS * TILES - 1, CHUNKS - 1, False)
                    copy_z(t)
                    relu(m1_ready, m1_copied, m1_sb, bt1_sb, t)
                    relu(m2_ready, m2_copied, m2_sb, bt2_sb, t)
                    copy_y(t)

            dve.sem_inc(top_free, 1)
            dve.wait_ge(front_loaded, 64)
            dve.tensor_copy(spread[:, :, :, :, F:FO].rearrange("p s g b o -> p (s g) (b o)"),
                            own_sb[:, :].rearrange("p (s b) -> p s b", s=1)
                            .to_broadcast([128, 2 * GROUPS, GB])).then_inc(constants_set, 1)
            dve.wait_ge(w0_loaded, 32)
            dve.tensor_tensor(w0_sb[:], w0ab_sb[:], w0ba_sb[:], ALU.add).then_inc(w0_added, 1)
            split(0, 0)
            split(0, 1)
            multiply(0, 0, True)
            spread_x(0, 0, True)
            over_tiles(dve, tile)

        @block.tensor
        def _(pe):
            def turn_parts(t, r):
                if r == 0:
                    for h in range(2):
                        pe.wait_ge(parts_done[h], t + 1)
                    if not (isinstance(t, int) and t == 0):
                        pe.wait_ge(x_spread, CHUNKS * t)
                else:
                    pe.wait_ge(turned_copied, 2 * t + 1)
                for d in range(8):
                    last = pe.transpose(x_bf[:, d * BT:(d + 1) * BT], parts_sb[:, 8 * r + d, :],
                                        ident_bf[:, :])
                last.then_inc(turned, 1)

            def columns(c):
                return parts_t[:, c * CB:(c + 1) * CB, :].rearrange("p b d -> p (b d)")

            def source(n, c, j, t_next, first):
                if c == 0 and j == 0:
                    pe.wait_ge(turned_copied, 2 * t_next + 2)
                if j >= 2:
                    pe.wait_ge(source_kept, KEPT * n + j - 1)
                    if j >= 3:
                        pe.wait_ge(multiplied, NP * n + USED_UP[j - 2])
                elif not first:
                    pe.wait_ge(multiplied, NP * (n - 1) + USED_UP[j + 3])
                pe.matmul(source_ps[(SOURCES * c + j) % 2][:, :], select_sb[:, j, :], columns(c),
                          start=True, stop=True).then_inc(selected, 1)

            def turn_x(n, c, first):
                if not first:
                    pe.wait_ge(x_spread, n)
                for g in range(GROUPS):
                    at = columns(c)[:, g * 128:(g + 1) * 128]
                    last = pe.matmul(x_ps[:, g * F:(g + 1) * F], at, select_t_sb[:, :], start=True, stop=True)
                last.then_inc(x_turned, 1)

            def layer1(n, c, k, first):
                if k == 0 and not first:
                    pe.wait_ge(h1_copied, n)
                pe.wait_ge(multiplied, NP * n + k + 1)
                last = pe.matmul(h1_ps[:, :], w0_sb[:, k, :], prods[:, c % 2, k, :], start=(k == 0),
                                 stop=(k == NP - 1))
                if k == NP - 1:
                    last.then_inc(h1_ready, 1)

            def turn_h1(n, c, first):
                pe.wait_ge(h1_copied, n + 1)
                if not first:
                    pe.wait_ge(h1t_copied, n)
                for g in range(GROUPS):
                    last = pe.transpose(h1t_ps[:, g, :], h1_sb[:, c % 2, g * 128:(g + 1) * 128], ident_sb[:, :])
                last.then_inc(h1_turned, 1)

            def sum_d(n, c, pair, first):
                if pair == 0:
                    pe.wait_ge(h1t_copied, n + 1)
                    pe.wait_ge(x_spread, n + 1)
                if not (first and pair == 0):
                    pe.wait_ge(gram_copied, 2 * n + pair)
                for g in range(2):
                    rhs = spread[:, c % 2, 2 * pair + g, :, :].rearrange("p b f -> p (b f)")
                    last = pe.matmul(gram_ps[:, g, 0:GB * FO], h1t_sb[:, c % 2, 2 * pair + g, :], rhs,
                                     start=True, stop=True)
                last.then_inc(gram_ready, 1)

            def layer2(t):
                pe.wait_ge(gram_copied, 2 * CHUNKS * (t + 1))
                pe.wait_ge(top_free, t + 1)
                for f in range(F):
                    last = pe.matmul(top_ps[:, 0:BT], w1_sb[:, f, :], gram[:, f, :], start=(f == 0),
                                     stop=(f == F - 1))
                last.then_inc(z2_ready, 1)

            def top1(t):
                pe.wait_ge(z_copied, 2 * (t + 1))
                for m in range(M1 // 128):
                    at, cols = top_ps[:, m * BT:(m + 1) * BT], slice(m * 128, (m + 1) * 128)
                    pe.matmul(at, wt1z_sb[:, 0, cols], z_sb[:, 0, :], start=True, stop=False)
                    pe.matmul(at, wt1z_sb[:, 1, cols], z_sb[:, 1, :], start=False, stop=False)
                    last = pe.matmul(at, wt1c_sb[:, cols], ctx_sb[:, bass.ds(t * BT, BT)], start=False, stop=True)
                last.then_inc(m1_ready, 1)

            def top2(t):
                pe.wait_ge(m1_copied, M1 // 128 * (t + 1))
                for m in range(M2 // 128):
                    for k in range(M1 // 128):
                        last = pe.matmul(top_ps[:, m * BT:(m + 1) * BT], wt2_sb[:, k, m * 128:(m + 1) * 128],
                                         m1_sb[:, k, :], start=(k == 0), stop=(k == M1 // 128 - 1))
                last.then_inc(m2_ready, 1)

            def top3(t):
                pe.wait_ge(m2_copied, M2 // 128 * (t + 1))
                for k in range(M2 // 128):
                    last = pe.matmul(top_ps[0:1, 0:BT], wt3_sb[:, k:k + 1], m2_sb[:, k, :], start=(k == 0),
                                     stop=(k == M2 // 128 - 1))
                last.then_inc(y_ready, 1)

            def tile(t, first, last):
                for c in range(CHUNKS):
                    n = CHUNKS * t + c
                    before, after = (c - 1) % CHUNKS, (c + 1) % CHUNKS
                    has_before, has_after = not (first and c == 0), not (last and c == CHUNKS - 1)
                    first_before = first and c == 1
                    turning = c == CHUNKS - 1 and not last

                    def next_source(j):
                        if has_after:
                            source(n + 1, after, j, t + 1, False)

                    if not first:
                        if c == 1:
                            layer2(t - 1)
                        elif c == 2:
                            top1(t - 1)
                        elif c == 3:
                            top2(t - 1)
                    if turning:
                        turn_parts(t + 1, 0)
                    layer1(n, c, 0, first and c == 0)
                    if turning:
                        turn_parts(t + 1, 1)
                    layer1(n, c, 1, False)
                    if has_before:
                        turn_h1(n - 1, before, first_before)
                    layer1(n, c, 2, False)
                    if c == 3 and not first:
                        top3(t - 1)
                    next_source(0)
                    next_source(1)
                    layer1(n, c, 3, False)
                    if has_before:
                        sum_d(n - 1, before, 0, first_before)
                    next_source(2)
                    layer1(n, c, 4, False)
                    next_source(3)
                    layer1(n, c, 5, False)
                    if has_after:
                        turn_x(n + 1, after, False)
                    layer1(n, c, 6, False)
                    next_source(4)
                    if has_before:
                        sum_d(n - 1, before, 1, False)
                if last:
                    turn_h1(n, c, False)
                    sum_d(n, c, 0, False)
                    sum_d(n, c, 1, False)
                    layer2(t)
                    top1(t)
                    top2(t)
                    top3(t)

            pe.wait_ge(constants_set, 4)
            pe.wait_ge(front_loaded, 64)
            turn_parts(0, 0)
            turn_parts(0, 1)
            for j in range(SOURCES):
                source(0, 0, j, 0, True)
            turn_x(0, 0, True)
            pe.wait_ge(w0_added, 1)
            pe.wait_ge(w1_loaded, 16)
            pe.wait_ge(top_loaded, 16 * 7)
            over_tiles(pe, tile)


def layouts(given):
    source = np.zeros((128, SOURCES), np.int64) - 1
    for i in range(SOURCES):
        for row, field in fields_of(i):
            source[row, i] = field
    w0 = np.concatenate([given["L0_rec_W0"].reshape(H, F * F), np.zeros((H, 1), np.float32)], axis=1)
    ab, ba = np.full((128, NP), F * F), np.full((128, NP), F * F)
    for k, (i, j) in enumerate(PAIRS):
        for row in range(128):
            a, b = source[row, i], source[row, j]
            if a >= 0 and b >= 0:
                ab[row, k] = a * F + b
                if a != b:
                    ba[row, k] = b * F + a
    select = np.zeros((PARTS, F, SOURCES, 128), np.float32)
    for i in range(SOURCES):
        for row, field in fields_of(i):
            select[:, field, i, row] = 1
    own = np.zeros((128, GB), np.float32)
    own[np.arange(128), np.arange(128) // D] = 1
    return {
        "ids": given["ids"],
        **{f"tbl_{f}": given[f"tbl_{f}"] for f in range(F)},
        "ctx_t": given["dense_ctx"].T,
        "w0_ab": w0.T[ab],
        "w0_ba": w0.T[ba],
        "w1": given["L0_rec_W1"].reshape(H, F, H).transpose(2, 1, 0),
        "select": select.reshape(PARTS * F, SOURCES, 128),
        "select_t": np.tile(np.eye(F, dtype=np.float32), (PARTS, 1)),
        "own": own,
        "ident": np.eye(128, dtype=np.float32),
        "w_top1z": given["W_top1"][:2 * H].reshape(2, H, M1).transpose(1, 0, 2),
        "w_top1c": given["W_top1"][2 * H:],
        "b_top1": given["b_top1"].reshape(M1 // 128, 128).T,
        "w_top2": given["W_top2"].reshape(M1 // 128, 128, M2).transpose(1, 0, 2),
        "b_top2": given["b_top2"].reshape(M2 // 128, 128).T,
        "w_top3": given["W_top3"].reshape(M2 // 128, 128).T,
    }


def kernel(**inputs):
    import concourse.bacc as bacc
    from concourse.bass_utils import run_bass_kernel_spmd

    nc = bacc.Bacc("TRN2", target_bir_lowering=False, num_devices=1)
    arrays = {n: np.ascontiguousarray(a) for n, a in layouts({n: np.asarray(a) for n, a in inputs.items()}).items()}
    args = {n: nc.dram_tensor(n, a.shape, mybir.dt.from_np(a.dtype), kind="ExternalInput").ap()
            for n, a in arrays.items()}
    tables = [args.pop(f"tbl_{f}") for f in range(F)]
    out = nc.dram_tensor("out", (BATCH, 1), mybir.dt.float32, kind="ExternalOutput").ap()
    build(nc, tables=tables, out=out, **args)
    r = run_bass_kernel_spmd(nc, [arrays], core_ids=[0])
    return r.results[0]["out"]
```

```python
import numpy as np
import concourse.bass as bass
from concourse import mybir
from contextlib import ExitStack

BATCH = 1024
F = 39
D = 16
H = 128
CTX = 16
M1, M2 = 512, 256

BT = 128
TILES = BATCH // BT
CB = 32
CHUNKS = BT // CB
COLS = CB * D
GROUPS = 4
GB = CB // GROUPS // 2
FO = F + 1

SHIFTS = ((0, 1, 6, 31), (0, 2, 12, 23), (0, 3, 7, 22))
LAST_SHIFTS = (0, 13)
SOURCES = 5
PAIRS = ((0, 1), (0, 2), (1, 2), (0, 3), (1, 3), (2, 3), (0, 4))
NP = len(PAIRS)
RUNS = tuple((j, min(k for k in range(NP) if PAIRS[k][1] == j), sum(p[1] == j for p in PAIRS))
             for j in range(1, SOURCES))
SPLIT_RUNS = 3
SPLIT = 6
KEPT = 3
PARTS = 3
HALF = (0, 20, F)


def fields_of(source):
    shifts = LAST_SHIFTS if source == 4 else [s[source] for s in SHIFTS]
    return [(F * g + p, (p + s) % F) for g, s in enumerate(shifts) for p in range(F)]


def build(nc, ids, tables, ctx_t, w0_ab, w0_ba, w1, select, select_t, own, ident, w_top1z, w_top1c,
          b_top1, w_top2, b_top2, w_top3, out):
    f32, f32r, bf16, i32 = mybir.dt.float32, mybir.dt.float32r, mybir.dt.bfloat16, mybir.dt.int32
    ALU, ACT = mybir.AluOpType, mybir.ActivationFunctionType

    with ExitStack() as stack:
        def sb(name, shape, dt=f32):
            return stack.enter_context(nc.sbuf_tensor(name, shape, dt))

        def ps(name, shape, dt=f32):
            return stack.enter_context(nc.psum_tensor(name, shape, dt))

        def sem(name):
            return stack.enter_context(nc.semaphore(name))

        w0ab_sb = sb("w0ab_sb", [128, NP, H])
        w0ba_sb = sb("w0ba_sb", [128, NP, H])
        w0_sb = sb("w0_sb", [128, NP, H])
        w0_hi = sb("w0_hi", [128, SPLIT, H], f32r)
        w0_lo = sb("w0_lo", [128, SPLIT, H], f32r)
        w1_sb = sb("w1_sb", [H, F, H])
        select_sb = sb("select_sb", [PARTS * F, SOURCES, 128], bf16)
        select_t_sb = sb("select_t_sb", [PARTS * F, F], bf16)
        select_f = sb("select_f", [PARTS * F, SOURCES, 128])
        select_t_f = sb("select_t_f", [PARTS * F, F])
        own_sb = sb("own_sb", [128, GB])
        ident_sb = sb("ident_sb", [128, 128])
        ident_bf = sb("ident_bf", [128, 128], bf16)
        wt1z_sb = sb("wt1z_sb", [128, 2, M1])
        wt1c_sb = sb("wt1c_sb", [CTX, M1])
        bt1_sb = sb("bt1_sb", [128, M1 // 128])
        wt2_sb = sb("wt2_sb", [128, M1 // 128, M2])
        bt2_sb = sb("bt2_sb", [128, M2 // 128])
        wt3_sb = sb("wt3_sb", [128, M2 // 128])
        ids_sb = [sb(f"ids_sb{h}", [BT, HALF[h + 1] - HALF[h]], i32) for h in range(2)]
        rows_sb = [sb(f"rows_sb{h}", [BT, HALF[h + 1] - HALF[h], D]) for h in range(2)]
        rest_sb = [sb(f"rest_sb{h}", [BT, HALF[h + 1] - HALF[h], D]) for h in range(2)]
        parts_sb = sb("parts_sb", [BT, D, PARTS * F], bf16)
        parts_t = sb("parts_t", [PARTS * F, BT, D], bf16)
        kept = sb("kept", [128, 2, KEPT, COLS])
        prods = sb("prods", [128, SPLIT, COLS])
        prods_hi = sb("prods_hi", [128, 2, SPLIT, COLS], f32r)
        prods_lo = sb("prods_lo", [128, 2, SPLIT, COLS], f32r)
        prods_whole = sb("prods_whole", [128, 2, NP - SPLIT, COLS])
        h1_sb = sb("h1_sb", [H, 2, COLS])
        h1t_sb = sb("h1t_sb", [128, 2, GROUPS, H])
        spread = sb("spread", [128, CHUNKS, GROUPS, GB, FO])
        gram = sb("gram", [H, FO, BT])
        z_sb = sb("z_sb", [128, 2, BT])
        ctx_sb = sb("ctx_sb", [CTX, BATCH])
        m1_sb = sb("m1_sb", [128, M1 // 128, BT])
        m2_sb = sb("m2_sb", [128, M2 // 128, BT])
        y_sb = sb("y_sb", [1, BATCH])

        source_ps = [ps(f"source_ps{i}", [128, COLS]) for i in range(2)]
        h1_ps = ps("h1_ps", [H, COLS])
        h1t_ps = ps("h1t_ps", [128, GROUPS, H])
        gram_ps = ps("gram_ps", [H, 2, 512])
        x_ps = ps("x_ps", [128, 512])
        top_ps = ps("top_ps", [128, 512])
        turned_ps = [x_ps[0:PARTS * F, :].bitcast(bf16),
                     h1t_ps[0:PARTS * F, :, :].rearrange("p g h -> p (g h)").bitcast(bf16)]

        ids_loaded = [sem(f"ids_loaded{h}") for h in range(2)]
        gathered = [sem(f"gathered{h}") for h in range(2)]
        front_loaded = sem("front_loaded")
        w0_loaded = sem("w0_loaded")
        w1_loaded = sem("w1_loaded")
        top_loaded = sem("top_loaded")
        y_stored = sem("y_stored")
        gathering = sem("gathering")
        w0_ready = sem("w0_ready")
        constants_set = sem("constants_set")
        first_part = [sem(f"first_part{h}") for h in range(2)]
        first_rest = [sem(f"first_rest{h}") for h in range(2)]
        second_part = [sem(f"second_part{h}") for h in range(2)]
        parts_done = sem("parts_done")
        turned = sem("turned")
        turned_copied = [sem(f"turned_copied{r}") for r in range(2)]
        selected = sem("selected")
        source_kept = sem("source_kept")
        multiplied = sem("multiplied")
        rounded = sem("rounded")
        rest_ready = sem("rest_ready")
        h1_ready = sem("h1_ready")
        h1_copied = sem("h1_copied")
        h1_turned = sem("h1_turned")
        h1t_copied = sem("h1t_copied")
        x_turned = sem("x_turned")
        x_spread = sem("x_spread")
        gram_ready = sem("gram_ready")
        gram_copied = sem("gram_copied")
        z2_ready = sem("z2_ready")
        z_copied = sem("z_copied")
        m1_ready = sem("m1_ready")
        m1_copied = sem("m1_copied")
        m2_ready = sem("m2_ready")
        m2_copied = sem("m2_copied")
        y_ready = sem("y_ready")
        top_free = sem("top_free")

        block = stack.enter_context(nc.Block())

        def over_tiles(eng, body):
            body(0, True, False)
            with eng.Fori(1, TILES - 1) as t:
                body(t, False, False)
            body(TILES - 1, False, True)

        @block.sync
        def _(sp):
            def load_ids(t, first):
                for h in range(2):
                    if not first:
                        sp.wait_ge(gathered[h], 16 * (HALF[h + 1] - HALF[h]) * t)
                    rows = ids.rearrange("(t p) f -> t p f", p=BT)[bass.ds(t, 1), :, HALF[h]:HALF[h + 1]]
                    sp.dma_start(ids_sb[h][:, :], rows.rearrange("t p f -> p (t f)"))\
                      .then_inc(ids_loaded[h], 16)

            load_ids(0, True)
            for to, of in ((select_f, select), (select_t_f, select_t), (own_sb, own)):
                sp.dma_start(to[:], of).then_inc(front_loaded, 16)
            sp.dma_start(w0ab_sb[:], w0_ab).then_inc(w0_loaded, 16)
            sp.dma_start(w0ba_sb[:], w0_ba).then_inc(w0_loaded, 16)
            sp.dma_start(w1_sb[:], w1).then_inc(w1_loaded, 16)
            for to, of in ((wt1z_sb, w_top1z), (wt1c_sb, w_top1c), (bt1_sb, b_top1), (wt2_sb, w_top2),
                           (bt2_sb, b_top2), (wt3_sb, w_top3), (ctx_sb, ctx_t)):
                sp.dma_start(to[:], of).then_inc(top_loaded, 16)

            with sp.Fori(1, TILES) as t:
                load_ids(t, False)
            sp.wait_ge(top_free, 1 + TILES)
            sp.dma_start(out.rearrange("(a b) o -> a (b o)", a=1), y_sb[:, :]).then_inc(y_stored, 16)
            sp.wait_ge(y_stored, 16)

        @block.gpsimd
        def _(pool):
            def gather(t, first):
                for h in range(2):
                    pool.wait_ge(ids_loaded[h], 16 * (t + 1))
                    if not first:
                        pool.wait_ge(first_rest[h], t)
                    pool.sem_inc(gathering, 1)
                    for f in range(HALF[h], HALF[h + 1]):
                        n = f - HALF[h]
                        pool.indirect_dma_start(
                            rows_sb[h][:, n, :], None, tables[f],
                            bass.IndirectOffsetOnAxis(ap=ids_sb[h][:, n:n + 1], axis=0),
                        ).then_inc(gathered[h], 16)

            gather(0, True)
            with pool.Fori(1, TILES) as t:
                gather(t, False)

        def part(which, h):
            lo = which * F
            return parts_sb[:, :, lo + HALF[h]:lo + HALF[h + 1]].rearrange("p d f -> p f d")

        @block.scalar
        def _(act):
            act.dma_start(ident_sb[:, :], ident).then_inc(front_loaded, 16)
            act.wait_ge(front_loaded, 64)
            for to, of in ((ident_bf, ident_sb), (select_sb, select_f), (select_t_sb, select_t_f)):
                act.activation(to[:], of[:], ACT.Copy).then_inc(constants_set, 1)

            def split(t, first):
                for h in range(2):
                    act.wait_ge(gathered[h], 16 * (HALF[h + 1] - HALF[h]) * (t + 1))
                    if h == 0 and not first:
                        act.wait_ge(turned, 2 * t)
                    act.activation(part(0, h), rows_sb[h][:, :, :], ACT.Copy).then_inc(first_part[h], 1)
                for h in range(2):
                    act.wait_ge(first_rest[h], t + 1)
                    act.activation(part(1, h), rest_sb[h][:, :, :], ACT.Copy).then_inc(second_part[h], 1)

            def copy_turned(t):
                act.wait_ge(turned, 2 * t + 1)
                act.activation(parts_t[:, :, 0:8], turned_ps[0].rearrange("p (d b) -> p b d", d=8),
                               ACT.Copy).then_inc(turned_copied[0], 1)

            def keep(n, c, j, first):
                act.wait_ge(selected, SOURCES * n + j + 1)
                if j == 0 and not first:
                    act.wait_ge(multiplied, len(RUNS) * (n - 1))
                act.activation(kept[:, c % 2, j, :], source_ps[(SOURCES * c + j) % 2][:, :], ACT.Copy)\
                   .then_inc(source_kept, 1)

            def round_products(n, c, r, first):
                _, k, many = RUNS[r]
                act.wait_ge(multiplied, len(RUNS) * n + r + 1)
                if r == 0 and not first:
                    act.wait_ge(h1_ready, n - 1)
                act.activation(prods_hi[:, c % 2, k:k + many, :], prods[:, k:k + many, :], ACT.Copy)\
                   .then_inc(rounded, 1)

            def copy_h1(n, c, first):
                act.wait_ge(h1_ready, n + 1)
                if not first:
                    act.wait_ge(h1_turned, n - 1)
                act.activation(h1_sb[:, c % 2, :], h1_ps[:, :], ACT.Copy).then_inc(h1_copied, 1)

            def copy_gram(n, c, pair, t):
                act.wait_ge(gram_ready, 2 * n + pair + 1)
                if c == 0 and pair == 0 and not (isinstance(t, int) and t == 0):
                    act.wait_ge(z_copied, 2 * t)
                to = gram[:, :, CB * c:CB * (c + 1)].rearrange("p f (s q) -> p f s q", s=2)
                act.activation(to[:, :, :, 2 * GB * pair:2 * GB * (pair + 1)],
                               gram_ps[:, :, 0:2 * GB * FO].rearrange("p s (b f) -> p f s b", f=FO), ACT.Copy)\
                   .then_inc(gram_copied, 1)

            def copy_h1t(n, c, first):
                act.wait_ge(h1_turned, n + 1)
                if not first:
                    act.wait_ge(gram_ready, 2 * (n - 1))
                act.activation(h1t_sb[:, c % 2, :, :], h1t_ps[:, :, :], ACT.Copy).then_inc(h1t_copied, 1)

            def tile(t, first, last):
                for c in range(CHUNKS):
                    n = CHUNKS * t + c
                    before, after = (c - 1) % CHUNKS, (c + 1) % CHUNKS
                    has_before, has_after = not (first and c == 0), not (last and c == CHUNKS - 1)
                    t_before = t - 1 if c == 0 else t
                    if has_after:
                        keep(n + 1, after, 0, first and c == 0)
                        keep(n + 1, after, 1, False)
                        keep(n + 1, after, 2, False)
                        round_products(n + 1, after, 0, first and c == 0)
                    if has_before:
                        copy_h1t(n - 1, before, first and c < 3)
                    if has_after:
                        round_products(n + 1, after, 1, False)
                    if has_before:
                        copy_gram(n - 1, before, 0, t_before)
                    if has_after:
                        round_products(n + 1, after, 2, False)
                    if c == CHUNKS - 2 and not last:
                        copy_turned(t + 1)
                    if has_before and c == 0:
                        copy_gram(n - 1, before, 1, t_before)
                    copy_h1(n, c, first and c < 2)
                    if c > 0:
                        copy_gram(n - 1, before, 1, t_before)
                    if c == 1 and not last:
                        split(t + 1, False)
                if last:
                    copy_h1t(n, c, False)
                    copy_gram(n, c, 0, t)
                    copy_gram(n, c, 1, t)

            split(0, True)
            copy_turned(0)
            keep(0, 0, 0, True)
            keep(0, 0, 1, True)
            round_products(0, 0, 0, True)
            keep(0, 0, 2, True)
            round_products(0, 0, 1, True)
            round_products(0, 0, 2, True)
            over_tiles(act, tile)

        @block.vector
        def _(dve):
            def split(t):
                for h in range(2):
                    dve.wait_ge(first_part[h], t + 1)
                    dve.tensor_tensor(rest_sb[h][:, :, :], rows_sb[h][:, :, :], part(0, h), ALU.subtract)\
                       .then_inc(first_rest[h], 1)
                for h in range(2):
                    dve.wait_ge(second_part[h], t + 1)
                    dve.tensor_tensor(part(2, h), rest_sb[h][:, :, :], part(1, h), ALU.subtract)\
                       .then_inc(parts_done, 1)

            def copy_turned(t):
                dve.wait_ge(turned, 2 * t + 2)
                dve.tensor_copy(parts_t[:, :, 8:16], turned_ps[1].rearrange("p (d b) -> p b d", d=8))\
                   .then_inc(turned_copied[1], 1)

            def multiply(n, c, r, first):
                j, k, many = RUNS[r]
                dve.wait_ge(selected, SOURCES * n + j + 1)
                dve.wait_ge(source_kept, KEPT * n + min(j, KEPT - 1) + 1)
                if r == 0 and not first:
                    dve.wait_ge(h1_ready, n - 1)
                if r < SPLIT_RUNS:
                    if not (isinstance(n, int) and n == 0):
                        dve.wait_ge(rest_ready, SPLIT_RUNS * (n - 1) + r + 1)
                    to = prods[:, k:k + many, :]
                else:
                    to = prods_whole[:, c % 2, k - SPLIT:k - SPLIT + many, :]
                one = source_ps[(SOURCES * c + j) % 2][:, :].rearrange("p (o x) -> p o x", o=1)
                dve.tensor_tensor(to, one.to_broadcast([128, many, COLS]), kept[:, c % 2, 0:many, :],
                                  ALU.mult).then_inc(multiplied, 1)

            def rest(n, c, r):
                _, k, many = RUNS[r]
                dve.wait_ge(rounded, SPLIT_RUNS * n + r + 1)
                dve.tensor_tensor(prods_lo[:, c % 2, k:k + many, :], prods[:, k:k + many, :],
                                  prods_hi[:, c % 2, k:k + many, :].bitcast(f32), ALU.subtract)\
                   .then_inc(rest_ready, 1)

            def spread_x(n, c, first):
                dve.wait_ge(x_turned, n + 1)
                if not first:
                    dve.wait_ge(gram_ready, 2 * (n - CHUNKS + 1))
                x = x_ps[:, 0:GROUPS * F].rearrange("p (g o f) -> p g o f", g=GROUPS, o=1)
                mask = own_sb[:, :].rearrange("p (g b f) -> p g b f", g=1, f=1)
                dve.tensor_tensor(spread[:, c, :, :, 0:F],
                                  x.to_broadcast([128, GROUPS, GB, F]),
                                  mask.to_broadcast([128, GROUPS, GB, F]), ALU.mult).then_inc(x_spread, 1)

            def copy_z(t):
                dve.wait_ge(z2_ready, t + 1)
                dve.tensor_copy(z_sb[:, 1, :], top_ps[:, 0:BT]).then_inc(z_copied, 1)
                dve.wait_ge(gram_copied, 2 * CHUNKS * (t + 1))
                dve.tensor_copy(z_sb[:, 0, :], gram[:, F, :]).then_inc(z_copied, 1)

            def relu(ready, copied, to, bias, t):
                dve.wait_ge(ready, t + 1)
                for m in range(to.shape[1]):
                    dve.tensor_scalar(to[:, m, :], top_ps[:, m * BT:(m + 1) * BT], bias[:, m:m + 1], 0.0,
                                      ALU.add, ALU.max).then_inc(copied, 1)

            def copy_y(t):
                dve.wait_ge(y_ready, t + 1)
                dve.tensor_copy(y_sb[:, bass.ds(t * BT, BT)], top_ps[0:1, 0:BT]).then_inc(top_free, 1)

            def tile(t, first, last):
                for c in range(CHUNKS):
                    n = CHUNKS * t + c
                    after, is_first = (c + 1) % CHUNKS, first and c == 0
                    has_after = not (last and c == CHUNKS - 1)
                    if has_after:
                        multiply(n + 1, after, 0, is_first)
                        multiply(n + 1, after, 1, False)
                        rest(n + 1, after, 0)
                    if not first:
                        if c == 1:
                            copy_z(t - 1)
                        elif c == 2:
                            relu(m1_ready, m1_copied, m1_sb, bt1_sb, t - 1)
                        elif c == 3:
                            relu(m2_ready, m2_copied, m2_sb, bt2_sb, t - 1)
                    if has_after:
                        spread_x(n + 1, after, first and c < CHUNKS - 1)
                        multiply(n + 1, after, 2, False)
                        rest(n + 1, after, 1)
                        multiply(n + 1, after, 3, False)
                    if c == CHUNKS - 2 and not last:
                        copy_turned(t + 1)
                    if has_after:
                        rest(n + 1, after, 2)
                    if c == 1 and not last:
                        split(t + 1)
                    if c == 3 and not first:
                        copy_y(t - 1)
                if last:
                    copy_z(t)
                    relu(m1_ready, m1_copied, m1_sb, bt1_sb, t)
                    relu(m2_ready, m2_copied, m2_sb, bt2_sb, t)
                    copy_y(t)

            dve.sem_inc(top_free, 1)
            dve.wait_ge(front_loaded, 64)
            dve.tensor_copy(spread[:, :, :, :, F:FO].rearrange("p s g b o -> p (s g) (b o)"),
                            own_sb[:, :].rearrange("p (s b) -> p s b", s=1)
                            .to_broadcast([128, CHUNKS * GROUPS, GB])).then_inc(constants_set, 1)
            dve.wait_ge(w0_loaded, 32)
            dve.tensor_tensor(w0_sb[:], w0ab_sb[:], w0ba_sb[:], ALU.add).then_inc(w0_ready, 1)
            dve.wait_ge(w0_ready, 1)
            dve.tensor_copy(w0_hi[:], w0_sb[:, 0:SPLIT, :]).then_inc(w0_ready, 1)
            dve.wait_ge(w0_ready, 2)
            dve.tensor_tensor(w0_lo[:], w0_sb[:, 0:SPLIT, :], w0_hi[:].bitcast(f32), ALU.subtract)\
               .then_inc(w0_ready, 1)
            split(0)
            copy_turned(0)
            multiply(0, 0, 0, True)
            multiply(0, 0, 1, True)
            rest(0, 0, 0)
            multiply(0, 0, 2, True)
            rest(0, 0, 1)
            multiply(0, 0, 3, True)
            spread_x(0, 0, True)
            rest(0, 0, 2)
            over_tiles(dve, tile)

        @block.tensor
        def _(pe):
            def turn_parts(t, first):
                pe.wait_ge(parts_done, 2 * (t + 1))
                if not first:
                    pe.wait_ge(x_spread, CHUNKS * t)
                    pe.wait_ge(h1t_copied, CHUNKS * t - 2)
                for r in range(2):
                    for d in range(8):
                        last = pe.transpose(turned_ps[r][:, d * BT:(d + 1) * BT], parts_sb[:, 8 * r + d, :],
                                            ident_bf[:, :])
                    last.then_inc(turned, 1)

            def columns(c):
                return parts_t[:, c * CB:(c + 1) * CB, :].rearrange("p b d -> p (b d)")

            def source(n, c, j, t_next, first):
                if c == 0 and j == 0:
                    for r in range(2):
                        pe.wait_ge(turned_copied[r], t_next + 1)
                if j >= 2:
                    pe.wait_ge(source_kept, KEPT * n + j - 1)
                    if j >= 3:
                        pe.wait_ge(multiplied, len(RUNS) * n + j - 2)
                elif not first:
                    pe.wait_ge(multiplied, len(RUNS) * (n - 1) + 3 + j)
                pe.matmul(source_ps[(SOURCES * c + j) % 2][:, :], select_sb[:, j, :], columns(c),
                          start=True, stop=True).then_inc(selected, 1)

            def turn_x(n, c, first):
                if not first:
                    pe.wait_ge(x_spread, n)
                for g in range(GROUPS):
                    at = columns(c)[:, g * 128:(g + 1) * 128]
                    last = pe.matmul(x_ps[:, g * F:(g + 1) * F], at, select_t_sb[:, :], start=True, stop=True)
                last.then_inc(x_turned, 1)

            def layer1(n, c, k, first):
                if k == 0 and not first:
                    pe.wait_ge(h1_copied, n)
                r = PAIRS[k][1] - 1
                if r < SPLIT_RUNS:
                    if k == RUNS[r][1]:
                        pe.wait_ge(rest_ready, SPLIT_RUNS * n + r + 1)
                    hi, lo = prods_hi[:, c % 2, k, :], prods_lo[:, c % 2, k, :]
                    pe.matmul(h1_ps[:, :], w0_hi[:, k, :], lo, start=(k == 0), stop=False)
                    pe.matmul(h1_ps[:, :], w0_hi[:, k, :], hi, start=False, stop=False)
                    last = pe.matmul(h1_ps[:, :], w0_lo[:, k, :], hi, start=False, stop=(k == NP - 1))
                else:
                    if k == RUNS[r][1]:
                        pe.wait_ge(multiplied, len(RUNS) * n + r + 1)
                    last = pe.matmul(h1_ps[:, :], w0_sb[:, k, :], prods_whole[:, c % 2, k - SPLIT, :],
                                     start=(k == 0), stop=(k == NP - 1))
                if k == NP - 1:
                    last.then_inc(h1_ready, 1)

            def turn_h1(n, c, first):
                pe.wait_ge(h1_copied, n + 1)
                if not first:
                    pe.wait_ge(h1t_copied, n)
                for g in range(GROUPS):
                    last = pe.transpose(h1t_ps[:, g, :], h1_sb[:, c % 2, g * 128:(g + 1) * 128], ident_sb[:, :])
                last.then_inc(h1_turned, 1)

            def sum_d(n, c, pair, first):
                if pair == 0:
                    pe.wait_ge(h1t_copied, n + 1)
                    pe.wait_ge(x_spread, n + 1)
                if not (first and pair == 0):
                    pe.wait_ge(gram_copied, 2 * n + pair)
                for g in range(2):
                    for s in range(2):
                        rows = slice(64 * s, 64 * (s + 1))
                        last = pe.matmul(
                            gram_ps[:, s, GB * FO * g:GB * FO * (g + 1)],
                            h1t_sb[rows, c % 2, 2 * pair + g, :],
                            spread[rows, c, 2 * pair + g, :, :].rearrange("p b f -> p (b f)"),
                            start=True, stop=True)
                last.then_inc(gram_ready, 1)

            def layer2(t, fields):
                if fields.start == 0:
                    pe.wait_ge(gram_copied, 2 * CHUNKS * (t + 1))
                    pe.wait_ge(top_free, t + 1)
                for f in range(F)[fields]:
                    last = pe.matmul(top_ps[:, 0:BT], w1_sb[:, f, :], gram[:, f, :], start=(f == 0),
                                     stop=(f == F - 1))
                if fields.stop == F:
                    last.then_inc(z2_ready, 1)

            def top1(t):
                pe.wait_ge(z_copied, 2 * (t + 1))
                for m in range(M1 // 128):
                    at, cols = top_ps[:, m * BT:(m + 1) * BT], slice(m * 128, (m + 1) * 128)
                    pe.matmul(at, wt1z_sb[:, 0, cols], z_sb[:, 0, :], start=True, stop=False)
                    pe.matmul(at, wt1z_sb[:, 1, cols], z_sb[:, 1, :], start=False, stop=False)
                    last = pe.matmul(at, wt1c_sb[:, cols], ctx_sb[:, bass.ds(t * BT, BT)], start=False, stop=True)
                last.then_inc(m1_ready, 1)

            def top2(t):
                pe.wait_ge(m1_copied, M1 // 128 * (t + 1))
                for m in range(M2 // 128):
                    for k in range(M1 // 128):
                        last = pe.matmul(top_ps[:, m * BT:(m + 1) * BT], wt2_sb[:, k, m * 128:(m + 1) * 128],
                                         m1_sb[:, k, :], start=(k == 0), stop=(k == M1 // 128 - 1))
                last.then_inc(m2_ready, 1)

            def top3(t):
                pe.wait_ge(m2_copied, M2 // 128 * (t + 1))
                for k in range(M2 // 128):
                    last = pe.matmul(top_ps[0:1, 0:BT], wt3_sb[:, k:k + 1], m2_sb[:, k, :], start=(k == 0),
                                     stop=(k == M2 // 128 - 1))
                last.then_inc(y_ready, 1)

            def tile(t, first, last):
                for c in range(CHUNKS):
                    n = CHUNKS * t + c
                    before, after = (c - 1) % CHUNKS, (c + 1) % CHUNKS
                    has_before, has_after = not (first and c == 0), not (last and c == CHUNKS - 1)
                    first_before = first and c == 1

                    def next_source(j):
                        if has_after:
                            source(n + 1, after, j, t + 1, False)

                    if c == 3 and not first:
                        top2(t - 1)
                    next_source(0)
                    next_source(1)
                    if c == 1 and not first:
                        layer2(t - 1, slice(F // 3, F))
                    if c == 2 and not first:
                        top1(t - 1)
                    layer1(n, c, 0, first and c == 0)
                    next_source(2)
                    layer1(n, c, 1, False)
                    if has_before:
                        turn_h1(n - 1, before, first_before)
                    next_source(3)
                    if has_after:
                        turn_x(n + 1, after, False)
                    layer1(n, c, 2, False)
                    layer1(n, c, 3, False)
                    if has_before:
                        sum_d(n - 1, before, 0, first_before)
                    next_source(4)
                    layer1(n, c, 4, False)
                    if c == CHUNKS - 2 and not last:
                        turn_parts(t + 1, False)
                    if c == 3 and not first:
                        top3(t - 1)
                    layer1(n, c, 5, False)
                    if c == 0:
                        if has_before:
                            sum_d(n - 1, before, 1, False)
                        layer1(n, c, 6, False)
                        if not first:
                            layer2(t - 1, slice(0, F // 3))
                    else:
                        layer1(n, c, 6, False)
                        sum_d(n - 1, before, 1, False)
                if last:
                    turn_h1(n, c, False)
                    sum_d(n, c, 0, False)
                    sum_d(n, c, 1, False)
                    layer2(t, slice(0, F))
                    top1(t)
                    top2(t)
                    top3(t)

            pe.wait_ge(constants_set, 4)
            pe.wait_ge(front_loaded, 64)
            turn_parts(0, True)
            for j in range(SOURCES):
                source(0, 0, j, 0, True)
            turn_x(0, 0, True)
            pe.wait_ge(w0_ready, 3)
            pe.wait_ge(w1_loaded, 16)
            pe.wait_ge(top_loaded, 16 * 7)
            over_tiles(pe, tile)


def layouts(given):
    source = np.zeros((128, SOURCES), np.int64) - 1
    for i in range(SOURCES):
        for row, field in fields_of(i):
            source[row, i] = field
    w0 = np.concatenate([given["L0_rec_W0"].reshape(H, F * F), np.zeros((H, 1), np.float32)], axis=1)
    ab, ba = np.full((128, NP), F * F), np.full((128, NP), F * F)
    for k, (i, j) in enumerate(PAIRS):
        for row in range(128):
            a, b = source[row, i], source[row, j]
            if a >= 0 and b >= 0:
                ab[row, k] = a * F + b
                if a != b:
                    ba[row, k] = b * F + a
    select = np.zeros((PARTS, F, SOURCES, 128), np.float32)
    for i in range(SOURCES):
        for row, field in fields_of(i):
            select[:, field, i, row] = 1
    own = np.zeros((128, GB), np.float32)
    own[np.arange(128), np.arange(128) // D % GB] = 1
    ids = given["ids"].reshape(TILES, CHUNKS, 2, GROUPS, GB, F).transpose(0, 1, 3, 2, 4, 5)
    return {
        "ids": ids.reshape(BATCH, F),
        **{f"tbl_{f}": given[f"tbl_{f}"] for f in range(F)},
        "ctx_t": given["dense_ctx"].T,
        "w0_ab": w0.T[ab],
        "w0_ba": w0.T[ba],
        "w1": given["L0_rec_W1"].reshape(H, F, H).transpose(2, 1, 0),
        "select": select.reshape(PARTS * F, SOURCES, 128),
        "select_t": np.tile(np.eye(F, dtype=np.float32), (PARTS, 1)),
        "own": own,
        "ident": np.eye(128, dtype=np.float32),
        "w_top1z": given["W_top1"][:2 * H].reshape(2, H, M1).transpose(1, 0, 2),
        "w_top1c": given["W_top1"][2 * H:],
        "b_top1": given["b_top1"].reshape(M1 // 128, 128).T,
        "w_top2": given["W_top2"].reshape(M1 // 128, 128, M2).transpose(1, 0, 2),
        "b_top2": given["b_top2"].reshape(M2 // 128, 128).T,
        "w_top3": given["W_top3"].reshape(M2 // 128, 128).T,
    }


def kernel(**inputs):
    import concourse.bacc as bacc
    from concourse.bass_utils import run_bass_kernel_spmd

    nc = bacc.Bacc("TRN2", target_bir_lowering=False, num_devices=1)
    arrays = {n: np.ascontiguousarray(a) for n, a in layouts({n: np.asarray(a) for n, a in inputs.items()}).items()}
    args = {n: nc.dram_tensor(n, a.shape, mybir.dt.from_np(a.dtype), kind="ExternalInput").ap()
            for n, a in arrays.items()}
    tables = [args.pop(f"tbl_{f}") for f in range(F)]
    out = nc.dram_tensor("out", (BATCH, 1), mybir.dt.float32, kind="ExternalOutput").ap()
    build(nc, tables=tables, out=out, **args)
    r = run_bass_kernel_spmd(nc, [arrays], core_ids=[0])
    return r.results[0]["out"]
```

```python
import numpy as np
import concourse.bass as bass
from concourse import mybir
from contextlib import ExitStack

BATCH = 1024
F = 39
D = 16
H = 128
CTX = 16
M1, M2 = 512, 256

BT = 128
TILES = BATCH // BT
CB = 32
CHUNKS = BT // CB
COLS = CB * D
GROUPS = 4
GB = CB // GROUPS // 2
FO = F + 1

SHIFTS = ((0, 1, 6, 31), (0, 2, 12, 23), (0, 3, 7, 22))
LAST_SHIFTS = (0, 13)
SOURCES = 5
PAIRS = ((0, 1), (0, 2), (1, 2), (0, 3), (1, 3), (2, 3), (0, 4))
NP = len(PAIRS)
RUNS = tuple((j, min(k for k in range(NP) if PAIRS[k][1] == j), sum(p[1] == j for p in PAIRS))
             for j in range(1, SOURCES))
KEPT = 3
PARTS = 3
HALF = (0, 18, F)
LOT = tuple(HALF[h + 1] - HALF[h] for h in range(2))
HOT_DEEP = 10
HOT_ROWS = 125
HOT_COLS = HOT_DEEP * D + 1
HOT_RUN = 512 // HOT_COLS
HOT_FIRST = LOT[0] // HOT_RUN
HOT_RUNS = HOT_FIRST + 3
HOT_NEXT = HOT_RUNS * HOT_RUN - LOT[0]
HOT = LOT[0] + HOT_NEXT


def whole(n, r):
    return r == len(RUNS) - 1 and isinstance(n, int) and n < CHUNKS


def split_runs(n):
    return len(RUNS) * n - (min(n, CHUNKS) if isinstance(n, int) else CHUNKS)


def fields_of(source):
    shifts = LAST_SHIFTS if source == 4 else [s[source] for s in SHIFTS]
    return [(F * g + p, (p + s) % F) for g, s in enumerate(shifts) for p in range(F)]


def build(nc, ids, hot_ids_given, hot_numbers, tables, ctx_t, w0_ab, w0_ba, w1, select, select_t, own, ident,
          w_top1z, w_top1c, b_top1, w_top2, b_top2, w_top3, out):
    f32, f32r, bf16, i32 = mybir.dt.float32, mybir.dt.float32r, mybir.dt.bfloat16, mybir.dt.int32
    ALU, ACT, AX = mybir.AluOpType, mybir.ActivationFunctionType, mybir.AxisListType

    with ExitStack() as stack:
        def sb(name, shape, dt=f32):
            return stack.enter_context(nc.sbuf_tensor(name, shape, dt))

        def ps(name, shape, dt=f32):
            return stack.enter_context(nc.psum_tensor(name, shape, dt))

        def sem(name):
            return stack.enter_context(nc.semaphore(name))

        w0ab_sb = sb("w0ab_sb", [128, NP, H])
        w0ba_sb = sb("w0ba_sb", [128, NP, H])
        w0_sb = sb("w0_sb", [128, NP, H])
        w0_hi = sb("w0_hi", [128, NP, H], f32r)
        w0_lo = sb("w0_lo", [128, NP, H], f32r)
        w1_sb = sb("w1_sb", [H, F, H])
        select_sb = sb("select_sb", [PARTS * F, SOURCES, 128], bf16)
        select_t_sb = sb("select_t_sb", [PARTS * F, F], bf16)
        select_f = sb("select_f", [PARTS * F, SOURCES, 128])
        select_t_f = sb("select_t_f", [PARTS * F, F])
        own_sb = sb("own_sb", [128, GB])
        ident_sb = sb("ident_sb", [128, 128])
        ident_bf = sb("ident_bf", [128, 128], bf16)
        wt1z_sb = sb("wt1z_sb", [128, 2, M1])
        wt1c_sb = sb("wt1c_sb", [CTX, M1])
        bt1_sb = sb("bt1_sb", [128, M1 // 128])
        wt2_sb = sb("wt2_sb", [128, M1 // 128, M2])
        bt2_sb = sb("bt2_sb", [128, M2 // 128])
        wt3_sb = sb("wt3_sb", [128, M2 // 128])
        ids_sb = [sb(f"ids_sb{h}", [BT, LOT[h]], i32) for h in range(2)]
        rows_sb = [sb(f"rows_sb{h}", [BT, LOT[h], D]) for h in range(2)]
        rest_sb = [sb(f"rest_sb{h}", [BT, LOT[h], D]) for h in range(2)]
        parts_sb = sb("parts_sb", [BT, D, PARTS * F], bf16)
        parts_t = sb("parts_t", [PARTS * F, BT, D], bf16)
        kept = sb("kept", [128, 2, KEPT, COLS])
        prods = sb("prods", [128, NP, COLS])
        prods_hi = sb("prods_hi", [128, 2, NP, COLS], f32r)
        prods_lo = sb("prods_lo", [128, 2, NP, COLS], f32r)
        prods_whole = sb("prods_whole", [128, 2, COLS])
        h1_sb = sb("h1_sb", [H, 2, COLS])
        h1t_sb = sb("h1t_sb", [128, 2, GROUPS, H])
        spread = sb("spread", [128, CHUNKS, GROUPS, GB, FO])
        gram = sb("gram", [H, FO, BT])
        z_sb = sb("z_sb", [128, 2, BT])
        ctx_sb = sb("ctx_sb", [CTX, BATCH])
        m1_sb = sb("m1_sb", [128, M1 // 128, BT])
        m2_sb = sb("m2_sb", [128, M2 // 128, BT])
        y_sb = sb("y_sb", [1, BATCH])

        hot_rows = [tables[f].shape[0] // HOT_DEEP for f in range(LOT[0])]
        assert all(HOT_DEEP * k == tables[f].shape[0] and k <= HOT_ROWS for f, k in enumerate(hot_rows))
        hot_tables = kept[0:HOT_ROWS].rearrange("p s j x -> p (s j x)")[:, 0:LOT[0] * HOT_COLS]\
            .rearrange("p (f x) -> p f x", x=HOT_COLS)
        hot_far = hot_ones = gram[0:HOT_ROWS, 0:HOT, :]
        hot_ids = hot_far.bitcast(i32)
        hot_within = sb("hot_within", [BT, HOT])
        hot_pick = sb("hot_pick", [BT, HOT, HOT_DEEP])
        hot_picked = [h1_sb[:, s, 0:HOT_RUN * HOT_DEEP * D].rearrange("p (f k d) -> p f k d", f=HOT_RUN, d=D)
                      for s in range(2)]
        hot_own_ids = sb("hot_own_ids", [BT, HOT], i32)
        hot_numbers_sb = sb("hot_numbers_sb", [128, 2 + HOT_DEEP])

        source_ps = [ps(f"source_ps{i}", [128, COLS]) for i in range(2)]
        h1_ps = ps("h1_ps", [H, COLS])
        h1t_ps = ps("h1t_ps", [128, GROUPS, H])
        gram_ps = ps("gram_ps", [H, 2, 512])
        x_ps = ps("x_ps", [128, 512])
        top_ps = ps("top_ps", [128, 512])
        last_m1_ps = [x_ps, h1_ps, h1t_ps.rearrange("p g h -> p (g h)"), gram_ps[:, 0]]
        last_m2_ps = [gram_ps[:, 1], source_ps[0]]
        turned_ps = [x_ps[0:PARTS * F, :].bitcast(bf16),
                     h1t_ps[0:PARTS * F, :, :].rearrange("p g h -> p (g h)").bitcast(bf16)]

        hot_ps = [bank[:, 0:HOT_RUN * HOT_COLS].rearrange("p (f x) -> p f x", x=HOT_COLS)
                  for bank in (gram_ps[:, 0], gram_ps[:, 1], top_ps, source_ps[0], source_ps[1], h1_ps)]

        hot_ids_loaded = sem("hot_ids_loaded")
        hot_loaded = [sem(f"hot_loaded{b}") for b in range(HOT_FIRST)]
        ids_loaded = [sem(f"ids_loaded{h}") for h in range(2)]
        gathered = [sem(f"gathered{h}") for h in range(2)]
        front_loaded = sem("front_loaded")
        w0_loaded = sem("w0_loaded")
        w1_loaded = sem("w1_loaded")
        top_loaded = sem("top_loaded")
        y_stored = sem("y_stored")
        gathering = sem("gathering")
        hot_numbered = sem("hot_numbered")
        hot_measured = sem("hot_measured")
        hot_made = sem("hot_made")
        hot_brought = sem("hot_brought")
        hot_within_ready = sem("hot_within_ready")
        hot_pick_ready = sem("hot_pick_ready")
        hot_picked_ready = sem("hot_picked_ready")
        hot_summed = sem("hot_summed")
        w0_ready = sem("w0_ready")
        constants_set = sem("constants_set")
        first_part = [sem(f"first_part{h}") for h in range(2)]
        first_rest = [sem(f"first_rest{h}") for h in range(2)]
        second_part = [sem(f"second_part{h}") for h in range(2)]
        parts_done = sem("parts_done")
        turned = sem("turned")
        turned_copied = [sem(f"turned_copied{r}") for r in range(2)]
        selected = sem("selected")
        source_kept = sem("source_kept")
        multiplied = sem("multiplied")
        rounded = sem("rounded")
        rest_ready = sem("rest_ready")
        h1_ready = sem("h1_ready")
        h1_copied = sem("h1_copied")
        h1_turned = sem("h1_turned")
        h1t_copied = sem("h1t_copied")
        x_turned = sem("x_turned")
        x_spread = sem("x_spread")
        gram_ready = sem("gram_ready")
        gram_copied = sem("gram_copied")
        gram_last = sem("gram_last")
        z2_ready = sem("z2_ready")
        z_copied = sem("z_copied")
        m1_ready = sem("m1_ready")
        m1_copied = sem("m1_copied")
        m2_ready = sem("m2_ready")
        m2_copied = sem("m2_copied")
        y_ready = sem("y_ready")
        top_free = sem("top_free")

        block = stack.enter_context(nc.Block())

        def source_bank(n, c, j):
            return top_ps if isinstance(n, int) and n == 0 and j == 2 else source_ps[(SOURCES * c + j) % 2]

        def over_tiles(eng, body):
            body(0, True, False)
            with eng.Fori(1, TILES - 1) as t:
                body(t, False, False)
            body(TILES - 1, False, True)

        def gathers(h, tiles):
            return 16 * (LOT[0] * (tiles - 1) - HOT_NEXT) if h == 0 else 16 * LOT[1] * tiles

        @block.sync
        def _(sp):
            def load_ids(t, h, free):
                if free is not None:
                    sp.wait_ge(gathered[h], gathers(h, free))
                rows = ids.rearrange("(t p) f -> t p f", p=BT)[bass.ds(t, 1), :, HALF[h]:HALF[h + 1]]
                sp.dma_start(ids_sb[h][:, :], rows.rearrange("t p f -> p (t f)"))\
                  .then_inc(ids_loaded[h], 16)

            load_ids(0, 1, None)
            sp.dma_start(hot_ids.rearrange("p f b -> p (f b)"),
                         hot_ids_given.rearrange("(o f) b -> o (f b)", o=1).to_broadcast([HOT_ROWS, HOT * BT]))\
              .then_inc(hot_ids_loaded, 16)
            sp.dma_start(hot_numbers_sb[:], hot_numbers).then_inc(hot_ids_loaded, 16)
            sp.dma_start(hot_own_ids[:, 0:LOT[0]], ids[0:BT, 0:LOT[0]]).then_inc(hot_ids_loaded, 16)
            sp.dma_start(hot_own_ids[:, LOT[0]:HOT], ids[BT:2 * BT, 0:HOT_NEXT]).then_inc(hot_ids_loaded, 16)
            for f in range(LOT[0]):
                sp.dma_start(hot_tables[0:hot_rows[f], f, 0:HOT_DEEP * D],
                             tables[f].rearrange("(p k) d -> p (k d)", k=HOT_DEEP))\
                  .then_inc(hot_loaded[f // HOT_RUN], 16)
            load_ids(1, 0, None)
            for to, of in ((select_f, select), (select_t_f, select_t), (own_sb, own)):
                sp.dma_start(to[:], of).then_inc(front_loaded, 16)
            sp.dma_start(w0ab_sb[:], w0_ab).then_inc(w0_loaded, 16)
            sp.dma_start(w0ba_sb[:], w0_ba).then_inc(w0_loaded, 16)
            for to, of in ((wt1z_sb, w_top1z), (wt1c_sb, w_top1c), (bt1_sb, b_top1), (wt2_sb, w_top2),
                           (bt2_sb, b_top2), (wt3_sb, w_top3), (ctx_sb, ctx_t)):
                sp.dma_start(to[:], of).then_inc(top_loaded, 16)
            sp.dma_start(w1_sb[:], w1).then_inc(w1_loaded, 16)

            load_ids(1, 1, 1)
            with sp.Fori(2, TILES) as t:
                load_ids(t, 0, t)
                load_ids(t, 1, t)
            sp.wait_ge(top_free, 1 + TILES)
            sp.dma_start(out.rearrange("(a b) o -> a (b o)", a=1), y_sb[:, :]).then_inc(y_stored, 16)
            sp.wait_ge(y_stored, 16)

        @block.gpsimd
        def _(pool):
            def gather(t, h, free, start=0):
                pool.wait_ge(ids_loaded[h], 16 * (t + h))
                if free is not None:
                    pool.wait_ge(first_rest[h], free)
                pool.sem_inc(gathering, 1)
                for f in range(HALF[h] + start, HALF[h + 1]):
                    n = f - HALF[h]
                    pool.indirect_dma_start(
                        rows_sb[h][:, n, :], None, tables[f],
                        bass.IndirectOffsetOnAxis(ap=ids_sb[h][:, n:n + 1], axis=0),
                    ).then_inc(gathered[h], 16)

            gather(0, 1, None)
            gather(1, 0, 1, HOT_NEXT)
            gather(1, 1, 1)
            with pool.Fori(2, TILES) as t:
                gather(t, 0, t)
                gather(t, 1, t)

        def part(which, h):
            lo = which * F
            return parts_sb[:, :, lo + HALF[h]:lo + HALF[h + 1]].rearrange("p d f -> p f d")

        @block.scalar
        def _(act):
            act.dma_start(ident_sb[:, :], ident).then_inc(front_loaded, 16)

            def split_first(t, first):
                for h in range(2):
                    if h == 1 or not first:
                        act.wait_ge(gathered[h], gathers(h, t + 1))
                    if h == 0 and isinstance(t, int) and t < 2:
                        act.wait_ge(hot_summed, (HOT_FIRST, HOT_RUNS)[t])
                    if h == 0 and not first:
                        act.wait_ge(turned, 2 * t)
                    act.activation(part(0, h), rows_sb[h][:, :, :], ACT.Copy).then_inc(first_part[h], 1)

            def split_second(t):
                for h in range(2):
                    act.wait_ge(first_rest[h], t + 1)
                    act.activation(part(1, h), rest_sb[h][:, :, :], ACT.Copy).then_inc(second_part[h], 1)

            def copy_turned(t):
                act.wait_ge(turned, 2 * t + 1)
                act.activation(parts_t[:, :, 0:8], turned_ps[0].rearrange("p (d b) -> p b d", d=8),
                               ACT.Copy).then_inc(turned_copied[0], 1)

            def keep(n, c, j, first):
                act.wait_ge(selected, SOURCES * n + j + 1)
                if j == 0 and not first:
                    act.wait_ge(multiplied, len(RUNS) * (n - 1))
                act.activation(kept[:, c % 2, j, :], source_bank(n, c, j)[:, :], ACT.Copy)\
                   .then_inc(source_kept, 1)

            def round_products(n, c, r, first):
                if whole(n, r):
                    return
                _, k, many = RUNS[r]
                act.wait_ge(multiplied, len(RUNS) * n + r + 1)
                if r == 0 and not first:
                    act.wait_ge(h1_ready, n - 1)
                act.activation(prods_hi[:, c % 2, k:k + many, :], prods[:, k:k + many, :], ACT.Copy)\
                   .then_inc(rounded, 1)

            def copy_h1(n, c, first):
                act.wait_ge(h1_ready, n + 1)
                if not first:
                    act.wait_ge(h1_turned, n - 1)
                act.activation(h1_sb[:, c % 2, :], h1_ps[:, :], ACT.Copy).then_inc(h1_copied, 1)

            def copy_gram(n, c, pair, t, banks=None):
                act.wait_ge(gram_ready, 2 * n + pair + 1)
                if c == 0 and pair == 0 and not (isinstance(t, int) and t == 0):
                    act.wait_ge(z_copied, 2 * t)
                to = gram[:, :, CB * c:CB * (c + 1)].rearrange("p f (s q) -> p f s q", s=2)
                to = to[:, :, :, 2 * GB * pair:2 * GB * (pair + 1)]
                if banks is None:
                    act.activation(to, gram_ps[:, :, 0:2 * GB * FO].rearrange("p s (b f) -> p f s b", f=FO),
                                   ACT.Copy).then_inc(gram_copied, 1)
                else:
                    act.activation(to[:, :, 0, :], banks[0][:, 0:2 * GB * FO].rearrange("p (b f) -> p f b", f=FO),
                                   ACT.Copy).then_inc(gram_copied, 1)

            def copy_h1t(n, c, first):
                act.wait_ge(h1_turned, n + 1)
                if not first:
                    act.wait_ge(gram_ready, 2 * (n - 1))
                act.activation(h1t_sb[:, c % 2, :, :], h1t_ps[:, :, :], ACT.Copy).then_inc(h1t_copied, 1)

            def tile(t, first, last):
                for c in range(CHUNKS):
                    n = CHUNKS * t + c
                    before, after = (c - 1) % CHUNKS, (c + 1) % CHUNKS
                    has_before, has_after = not (first and c == 0), not (last and c == CHUNKS - 1)
                    t_before = t - 1 if c == 0 else t
                    if has_after:
                        if c == 3 or first and c == 0:
                            keep(n + 1, after, 0, first and c == 0)
                        keep(n + 1, after, 1, False)
                    if not (first and c < 2) and c != 1:
                        copy_gram(n - 2, (c - 2) % CHUNKS, 1, None)
                    if has_after:
                        keep(n + 1, after, 2, False)
                        round_products(n + 1, after, 0, first and c == 0)
                    if has_before:
                        copy_h1t(n - 1, before, first and c < 3)
                    if has_after:
                        round_products(n + 1, after, 1, False)
                    if c == 1 and not last:
                        split_first(t + 1, False)
                    if has_before:
                        copy_gram(n - 1, before, 0, t_before)
                    if c == 2 and not last:
                        copy_turned(t + 1)
                    if has_after:
                        round_products(n + 1, after, 2, False)
                    if has_before and c == 0:
                        copy_gram(n - 1, before, 1, t_before)
                    if c == 3 and has_after:
                        round_products(n + 1, after, 3, False)
                    if c > 0:
                        copy_h1(n, c, first and c < 2)
                    if c == 1 and not last:
                        split_second(t + 1)
                    if c != 2 and not (last and c == 3):
                        keep(n + 2, (c + 2) % CHUNKS, 0, False)
                    if has_after and c < 3:
                        round_products(n + 1, after, 3, False)
                    if c == 0:
                        copy_h1(n, c, first)
                    elif last and c == 3:
                        copy_gram(n - 1, before, 1, t_before)
                if last:
                    copy_h1t(n, c, False)
                    copy_gram(n, c, 0, t)
                    copy_gram(n, c, 1, t, source_ps)

            act.wait_ge(hot_ids_loaded, 64)
            for s in range(3):
                fields = slice(s * HOT // 3, (s + 1) * HOT // 3)
                act.activation(hot_far[:, fields, :], hot_ids[:, fields, :], ACT.Square,
                               bias=hot_numbers_sb[0:HOT_ROWS, 0:1]).then_inc(hot_measured, 1)

            act.wait_ge(front_loaded, 64)
            for to, of in ((ident_bf, ident_sb), (select_sb, select_f), (select_t_sb, select_t_f)):
                act.activation(to[:], of[:], ACT.Copy).then_inc(constants_set, 1)
            split_first(0, True)
            split_second(0)
            copy_turned(0)
            keep(0, 0, 0, True)
            keep(0, 0, 1, True)
            keep(0, 0, 2, True)
            round_products(0, 0, 0, True)
            round_products(0, 0, 1, True)
            round_products(0, 0, 2, True)
            round_products(0, 0, 3, True)
            over_tiles(act, tile)

        @block.vector
        def _(dve):
            def split_first(t, h):
                dve.wait_ge(first_part[h], t + 1)
                dve.tensor_tensor(rest_sb[h][:, :, :], rows_sb[h][:, :, :], part(0, h), ALU.subtract)\
                   .then_inc(first_rest[h], 1)

            def split_second(t):
                for h in range(2):
                    dve.wait_ge(second_part[h], t + 1)
                    dve.tensor_tensor(part(2, h), rest_sb[h][:, :, :], part(1, h), ALU.subtract)\
                       .then_inc(parts_done, 1)

            def copy_turned(t):
                dve.wait_ge(turned, 2 * t + 2)
                dve.tensor_copy(parts_t[:, :, 8:16], turned_ps[1].rearrange("p (d b) -> p b d", d=8))\
                   .then_inc(turned_copied[1], 1)

            def multiply(n, c, r):
                j, k, many = RUNS[r]
                dve.wait_ge(selected, SOURCES * n + j + 1)
                dve.wait_ge(source_kept, KEPT * n + min(j, KEPT - 1) + 1)
                to = prods[:, k:k + many, :]
                if whole(n, r):
                    to = prods_whole[:, c % 2:c % 2 + many, :]
                    if n >= 2:
                        dve.wait_ge(h1_ready, n - 1)
                elif not (isinstance(n, int) and n == 0) and not whole(n - 1, r):
                    dve.wait_ge(rest_ready, split_runs(n - 1) + r + 1)
                one = source_bank(n, c, j)[:, :].rearrange("p (o x) -> p o x", o=1)
                dve.tensor_tensor(to, one.to_broadcast([128, many, COLS]), kept[:, c % 2, 0:many, :],
                                  ALU.mult).then_inc(multiplied, 1)

            def rest(n, c, r):
                if whole(n, r):
                    return
                _, k, many = RUNS[r]
                dve.wait_ge(rounded, split_runs(n) + r + 1)
                dve.tensor_tensor(prods_lo[:, c % 2, k:k + many, :], prods[:, k:k + many, :],
                                  prods_hi[:, c % 2, k:k + many, :].bitcast(f32), ALU.subtract)\
                   .then_inc(rest_ready, 1)

            def spread_x(n, c, first):
                dve.wait_ge(x_turned, n + 1)
                if not first:
                    dve.wait_ge(gram_ready, 2 * (n - CHUNKS + 1))
                x = x_ps[:, 0:GROUPS * F].rearrange("p (g o f) -> p g o f", g=GROUPS, o=1)
                mask = own_sb[:, :].rearrange("p (g b f) -> p g b f", g=1, f=1)
                dve.tensor_tensor(spread[:, c, :, :, 0:F],
                                  x.to_broadcast([128, GROUPS, GB, F]),
                                  mask.to_broadcast([128, GROUPS, GB, F]), ALU.mult).then_inc(x_spread, 1)

            def copy_z(t):
                dve.wait_ge(z2_ready, t + 1)
                dve.tensor_copy(z_sb[:, 1, :], top_ps[:, 0:BT]).then_inc(z_copied, 1)
                dve.wait_ge(gram_copied, 2 * CHUNKS * (t + 1))
                dve.tensor_copy(z_sb[:, 0, :], gram[:, F, :]).then_inc(z_copied, 1)

            def relu(ready, copied, to, bias, t):
                dve.wait_ge(ready, t + 1)
                for m in range(to.shape[1]):
                    dve.tensor_scalar(to[:, m, :], top_ps[:, m * BT:(m + 1) * BT], bias[:, m:m + 1], 0.0,
                                      ALU.add, ALU.max).then_inc(copied, 1)

            def relu_blocks(ready, copied, to, bias, banks, t):
                for m in range(to.shape[1]):
                    dve.wait_ge(ready, t + 1 + m)
                    dve.tensor_scalar(to[:, m, :], banks[m][:, 0:BT], bias[:, m:m + 1], 0.0,
                                      ALU.add, ALU.max).then_inc(copied, 1)

            def copy_y(t):
                dve.wait_ge(y_ready, t + 1)
                dve.tensor_copy(y_sb[:, bass.ds(t * BT, BT)], top_ps[0:1, 0:BT]).then_inc(top_free, 1)

            def tile(t, first, last):
                for c in range(CHUNKS):
                    n = CHUNKS * t + c
                    after = (c + 1) % CHUNKS
                    has_after = not (last and c == CHUNKS - 1)
                    if has_after:
                        multiply(n + 1, after, 0)
                        multiply(n + 1, after, 1)
                        rest(n + 1, after, 0)
                    if not first:
                        if c == 1:
                            copy_z(t - 1)
                        elif c == 3:
                            relu(m2_ready, m2_copied, m2_sb, bt2_sb, t - 1)
                    if has_after:
                        spread_x(n + 1, after, first and c < CHUNKS - 1)
                        multiply(n + 1, after, 2)
                        rest(n + 1, after, 1)
                    if c == CHUNKS - 2 and not last:
                        copy_turned(t + 1)
                    if has_after:
                        multiply(n + 1, after, 3)
                    if c == 1 and not last:
                        split_first(t + 1, 0)
                        split_first(t + 1, 1)
                    if c == 2 and not first:
                        relu(m1_ready, m1_copied, m1_sb, bt1_sb, t - 1)
                    if has_after:
                        rest(n + 1, after, 2)
                        rest(n + 1, after, 3)
                    if c == 1 and not last:
                        split_second(t + 1)
                    if c == 3 and not first and not last:
                        copy_y(t - 1)
                if last:
                    dve.wait_ge(gram_ready, 2 * n + 2)
                    dve.tensor_copy(gram[:, :, CB * c + CB - 2 * GB:CB * (c + 1)],
                                    source_ps[1][:, 0:2 * GB * FO].rearrange("p (b f) -> p f b", f=FO))\
                       .then_inc(gram_last, 1)
                    copy_y(t - 1)
                    dve.wait_ge(gram_last, 1)
                    dve.wait_ge(gram_copied, 2 * CHUNKS * (t + 1))
                    dve.tensor_copy(z_sb[:, 0, :], gram[:, F, :]).then_inc(z_copied, 1)
                    dve.wait_ge(z2_ready, t + 1)
                    dve.tensor_copy(z_sb[:, 1, :], top_ps[:, 0:BT]).then_inc(z_copied, 1)
                    relu_blocks(m1_ready, m1_copied, m1_sb, bt1_sb, last_m1_ps, t)
                    relu_blocks(m2_ready, m2_copied, m2_sb, bt2_sb, last_m2_ps, t)
                    copy_y(t)

            def hot_ones_of(s):
                fields = slice(s * HOT // 3, (s + 1) * HOT // 3)
                dve.wait_ge(hot_measured, s + 1)
                dve.tensor_scalar(hot_ones[:, fields, :], hot_far[:, fields, :], HOT_DEEP ** 2 / 4, None,
                                  ALU.is_lt).then_inc(hot_made, 1)

            def hot_rows_of(b):
                fields = slice(b * HOT_RUN, (b + 1) * HOT_RUN)
                bank = hot_ps[b % HOT_FIRST]
                dve.wait_ge(hot_brought, b + 1)
                dve.tensor_tensor(hot_within[:, fields], hot_own_ids[:, fields],
                                  bank[:, :, HOT_COLS - 1], ALU.subtract).then_inc(hot_within_ready, 1)
                dve.wait_ge(hot_within_ready, b + 1)
                one = hot_within[:, fields].rearrange("p (f k) -> p f k", k=1)
                number = hot_numbers_sb[:, 2:2 + HOT_DEEP].rearrange("p (f k) -> p f k", f=1)
                shape = [BT, HOT_RUN, HOT_DEEP]
                dve.tensor_tensor(hot_pick[:, fields, :], one.to_broadcast(shape), number.to_broadcast(shape),
                                  ALU.is_equal).then_inc(hot_pick_ready, 1)
                dve.wait_ge(hot_pick_ready, b + 1)
                if b >= 2:
                    dve.wait_ge(hot_summed, b - 1)
                dve.tensor_tensor(hot_picked[b % 2],
                                  bank[:, :, 0:HOT_DEEP * D].rearrange("p f (k d) -> p f k d", d=D),
                                  hot_pick[:, fields, :].rearrange("p f (k o) -> p f k o", o=1)
                                  .to_broadcast([BT, HOT_RUN, HOT_DEEP, D]), ALU.mult)\
                   .then_inc(hot_picked_ready, 1)
                dve.wait_ge(hot_picked_ready, b + 1)
                at = HOT_RUN * (b % HOT_FIRST)
                if b == HOT_FIRST:
                    dve.wait_ge(first_rest[0], 1)
                dve.tensor_reduce(rows_sb[0][:, at:at + HOT_RUN, :], hot_picked[b % 2].rearrange("p f k d -> p f d k"),
                                  AX.X, ALU.add).then_inc(hot_summed, 1)

            dve.sem_inc(top_free, 1)
            for s in range(3):
                hot_ones_of(s)
                if s == 0:
                    dve.tensor_copy(hot_tables[:, :, HOT_COLS - 1],
                                    hot_numbers_sb[0:HOT_ROWS, 1:2].to_broadcast([HOT_ROWS, LOT[0]]))\
                       .then_inc(hot_numbered, 1)
            for b in range(HOT_FIRST):
                hot_rows_of(b)
            dve.wait_ge(front_loaded, 64)
            dve.tensor_copy(spread[:, :, :, :, F:FO].rearrange("p s g b o -> p (s g) (b o)"),
                            own_sb[:, :].rearrange("p (s b) -> p s b", s=1)
                            .to_broadcast([128, CHUNKS * GROUPS, GB])).then_inc(constants_set, 1)
            split_first(0, 0)
            for b in range(HOT_FIRST, HOT_RUNS):
                hot_rows_of(b)
            dve.wait_ge(w0_loaded, 32)
            dve.tensor_tensor(w0_sb[:], w0ab_sb[:], w0ba_sb[:], ALU.add).then_inc(w0_ready, 1)
            split_first(0, 1)
            split_second(0)
            dve.wait_ge(w0_ready, 1)
            dve.tensor_copy(w0_hi[:], w0_sb[:]).then_inc(w0_ready, 1)
            copy_turned(0)
            dve.wait_ge(w0_ready, 2)
            dve.tensor_tensor(w0_lo[:], w0_sb[:], w0_hi[:].bitcast(f32), ALU.subtract)\
               .then_inc(w0_ready, 1)
            multiply(0, 0, 0)
            multiply(0, 0, 1)
            rest(0, 0, 0)
            multiply(0, 0, 2)
            rest(0, 0, 1)
            multiply(0, 0, 3)
            spread_x(0, 0, True)
            rest(0, 0, 2)
            rest(0, 0, 3)
            over_tiles(dve, tile)

        @block.tensor
        def _(pe):
            def turn_parts(t, first):
                pe.wait_ge(parts_done, 2 * (t + 1))
                if not first:
                    pe.wait_ge(x_spread, CHUNKS * t)
                    pe.wait_ge(h1t_copied, CHUNKS * t - 2)
                for r in range(2):
                    for d in range(8):
                        last = pe.transpose(turned_ps[r][:, d * BT:(d + 1) * BT], parts_sb[:, 8 * r + d, :],
                                            ident_bf[:, :])
                    last.then_inc(turned, 1)

            def columns(c):
                return parts_t[:, c * CB:(c + 1) * CB, :].rearrange("p b d -> p (b d)")

            def source(n, c, j, t_next, first):
                if c == 0 and j == 0:
                    for r in range(2):
                        pe.wait_ge(turned_copied[r], t_next + 1)
                if first:
                    if j == 2:
                        pe.wait_ge(hot_picked_ready, HOT_RUNS)
                    elif j == 3:
                        pe.wait_ge(source_kept, 2)
                        pe.wait_ge(multiplied, 1)
                    elif j == 4:
                        pe.wait_ge(source_kept, 1)
                elif j >= 2:
                    pe.wait_ge(source_kept, KEPT * n + j - 1)
                    if j >= 3:
                        pe.wait_ge(multiplied, len(RUNS) * n + j - 2)
                else:
                    pe.wait_ge(multiplied, len(RUNS) * (n - 1) + 3 + j)
                pe.matmul(source_bank(n, c, j)[:, :], select_sb[:, j, :], columns(c),
                          start=True, stop=True).then_inc(selected, 1)

            def turn_x(n, c, first):
                if not first:
                    pe.wait_ge(x_spread, n)
                for g in range(GROUPS):
                    at = columns(c)[:, g * 128:(g + 1) * 128]
                    last = pe.matmul(x_ps[:, g * F:(g + 1) * F], at, select_t_sb[:, :], start=True, stop=True)
                last.then_inc(x_turned, 1)

            def layer1(n, c, k, first):
                if k == 0 and not first:
                    pe.wait_ge(h1_copied, n)
                r = PAIRS[k][1] - 1
                if whole(n, r):
                    pe.wait_ge(multiplied, len(RUNS) * n + r + 1)
                    pe.matmul(h1_ps[:, :], w0_sb[:, k, :], prods_whole[:, c % 2, :], start=False, stop=True)\
                      .then_inc(h1_ready, 1)
                    return
                if k == RUNS[r][1]:
                    pe.wait_ge(rest_ready, split_runs(n) + r + 1)
                hi, lo = prods_hi[:, c % 2, k, :], prods_lo[:, c % 2, k, :]
                pe.matmul(h1_ps[:, :], w0_hi[:, k, :], lo, start=(k == 0), stop=False)
                pe.matmul(h1_ps[:, :], w0_hi[:, k, :], hi, start=False, stop=False)
                last = pe.matmul(h1_ps[:, :], w0_lo[:, k, :], hi, start=False, stop=(k == NP - 1))
                if k == NP - 1:
                    last.then_inc(h1_ready, 1)

            def turn_h1(n, c, first):
                pe.wait_ge(h1_copied, n + 1)
                if not first:
                    pe.wait_ge(h1t_copied, n)
                for g in range(GROUPS):
                    last = pe.transpose(h1t_ps[:, g, :], h1_sb[:, c % 2, g * 128:(g + 1) * 128], ident_sb[:, :])
                last.then_inc(h1_turned, 1)

            def sum_d(n, c, pair, first, banks=None):
                if pair == 0:
                    pe.wait_ge(h1t_copied, n + 1)
                    pe.wait_ge(x_spread, n + 1)
                if banks is not None:
                    pe.wait_ge(multiplied, len(RUNS) * (n + 1))
                elif not (first and pair == 0):
                    pe.wait_ge(gram_copied, 2 * n + pair)
                for g in range(2):
                    for s in range(2):
                        rows = slice(64 * s, 64 * (s + 1))
                        last = pe.matmul(
                            (gram_ps[:, s] if banks is None else banks[s])[:, GB * FO * g:GB * FO * (g + 1)],
                            h1t_sb[rows, c % 2, 2 * pair + g, :],
                            spread[rows, c, 2 * pair + g, :, :].rearrange("p b f -> p (b f)"),
                            start=True, stop=True)
                last.then_inc(gram_ready, 1)

            def layer2(t, fields):
                if fields.start == 0:
                    pe.wait_ge(gram_copied, 2 * CHUNKS * (t + 1))
                    if isinstance(t, int) and t == TILES - 1:
                        pe.wait_ge(gram_last, 1)
                    pe.wait_ge(top_free, t + 1)
                for f in range(F)[fields]:
                    last = pe.matmul(top_ps[:, 0:BT], w1_sb[:, f, :], gram[:, f, :], start=(f == 0),
                                     stop=(f == F - 1))
                if fields.stop == F:
                    last.then_inc(z2_ready, 1)

            def top1(t):
                pe.wait_ge(z_copied, 2 * (t + 1))
                for m in range(M1 // 128):
                    at, cols = top_ps[:, m * BT:(m + 1) * BT], slice(m * 128, (m + 1) * 128)
                    pe.matmul(at, wt1z_sb[:, 0, cols], z_sb[:, 0, :], start=True, stop=False)
                    pe.matmul(at, wt1z_sb[:, 1, cols], z_sb[:, 1, :], start=False, stop=False)
                    last = pe.matmul(at, wt1c_sb[:, cols], ctx_sb[:, bass.ds(t * BT, BT)], start=False, stop=True)
                last.then_inc(m1_ready, 1)

            def top2(t):
                pe.wait_ge(m1_copied, M1 // 128 * (t + 1))
                for m in range(M2 // 128):
                    for k in range(M1 // 128):
                        last = pe.matmul(top_ps[:, m * BT:(m + 1) * BT], wt2_sb[:, k, m * 128:(m + 1) * 128],
                                         m1_sb[:, k, :], start=(k == 0), stop=(k == M1 // 128 - 1))
                last.then_inc(m2_ready, 1)

            def top3(t):
                pe.wait_ge(m2_copied, M2 // 128 * (t + 1))
                for k in range(M2 // 128):
                    last = pe.matmul(top_ps[0:1, 0:BT], wt3_sb[:, k:k + 1], m2_sb[:, k, :], start=(k == 0),
                                     stop=(k == M2 // 128 - 1))
                last.then_inc(y_ready, 1)

            def last_top(t):
                pe.wait_ge(z_copied, 2 * t + 1)
                for m in range(M1 // 128):
                    at, cols = last_m1_ps[m][:, 0:BT], slice(m * 128, (m + 1) * 128)
                    pe.matmul(at, wt1z_sb[:, 0, cols], z_sb[:, 0, :], start=True, stop=False)
                    pe.matmul(at, wt1c_sb[:, cols], ctx_sb[:, bass.ds(t * BT, BT)], start=False, stop=False)
                pe.wait_ge(z_copied, 2 * t + 2)
                for m in range(M1 // 128):
                    pe.matmul(last_m1_ps[m][:, 0:BT], wt1z_sb[:, 1, m * 128:(m + 1) * 128], z_sb[:, 1, :],
                              start=False, stop=True).then_inc(m1_ready, 1)
                for k in range(M1 // 128):
                    pe.wait_ge(m1_copied, M1 // 128 * t + k + 1)
                    for m in range(M2 // 128):
                        last = pe.matmul(last_m2_ps[m][:, 0:BT], wt2_sb[:, k, m * 128:(m + 1) * 128],
                                         m1_sb[:, k, :], start=(k == 0), stop=(k == M1 // 128 - 1))
                        if k == M1 // 128 - 1:
                            last.then_inc(m2_ready, 1)
                for k in range(M2 // 128):
                    pe.wait_ge(m2_copied, M2 // 128 * t + k + 1)
                    last = pe.matmul(top_ps[0:1, 0:BT], wt3_sb[:, k:k + 1], m2_sb[:, k, :], start=(k == 0),
                                     stop=(k == M2 // 128 - 1))
                last.then_inc(y_ready, 1)

            def tile(t, first, last):
                for c in range(CHUNKS):
                    n = CHUNKS * t + c
                    before, after = (c - 1) % CHUNKS, (c + 1) % CHUNKS
                    has_before, has_after = not (first and c == 0), not (last and c == CHUNKS - 1)
                    first_before = first and c == 1

                    def next_source(j):
                        if has_after:
                            source(n + 1, after, j, t + 1, False)

                    if c == 3 or first and c == 0:
                        next_source(0)
                    next_source(1)
                    layer1(n, c, 0, first and c == 0)
                    next_source(2)
                    if c == 1 and not first:
                        layer2(t - 1, slice(F // 3, F))
                    if c == 2 and not first:
                        top1(t - 1)
                    if c == 3 and not first and not last:
                        top2(t - 1)
                    layer1(n, c, 1, False)
                    if has_before:
                        turn_h1(n - 1, before, first_before)
                    next_source(3)
                    if has_after:
                        turn_x(n + 1, after, False)
                    layer1(n, c, 2, False)
                    layer1(n, c, 3, False)
                    if has_before:
                        sum_d(n - 1, before, 0, first_before)
                    next_source(4)
                    if c == CHUNKS - 2 and not last:
                        turn_parts(t + 1, False)
                    layer1(n, c, 4, False)
                    if c == 0 and has_before:
                        sum_d(n - 1, before, 1, False)
                    if c == 3 and not first and not last:
                        top3(t - 1)
                    layer1(n, c, 5, False)
                    if c != 2 and not (last and c == 3):
                        source(n + 2, (c + 2) % CHUNKS, 0, None, False)
                    if c == 0:
                        layer1(n, c, 6, False)
                        if not first:
                            layer2(t - 1, slice(0, F // 3))
                    else:
                        layer1(n, c, 6, False)
                        sum_d(n - 1, before, 1, False)
                if last:
                    turn_h1(n, c, False)
                    top2(t - 1)
                    sum_d(n, c, 0, False)
                    sum_d(n, c, 1, False, source_ps)
                    top3(t - 1)
                    layer2(t, slice(0, F))
                    last_top(t)

            pe.wait_ge(hot_numbered, 1)
            for b in range(HOT_RUNS):
                if b < HOT_FIRST:
                    pe.wait_ge(hot_loaded[b], 16 * HOT_RUN)
                else:
                    pe.wait_ge(hot_picked_ready, b - HOT_FIRST + 1)
                pe.wait_ge(hot_made, 1 + b * 3 // HOT_RUNS)
                for n in range(HOT_RUN):
                    i = b * HOT_RUN + n
                    f = i % LOT[0]
                    last = pe.matmul(hot_ps[b % HOT_FIRST][:, n, :], hot_ones[0:hot_rows[f], i, :],
                                     hot_tables[0:hot_rows[f], f, :], start=True, stop=True)
                last.then_inc(hot_brought, 1)
            turn_parts(0, True)
            for j in range(SOURCES):
                source(0, 0, j, 0, True)
            turn_x(0, 0, True)
            pe.wait_ge(hot_summed, HOT_RUNS)
            pe.wait_ge(w0_ready, 3)
            pe.wait_ge(w1_loaded, 16)
            pe.wait_ge(top_loaded, 16 * 7)
            over_tiles(pe, tile)


def layouts(given):
    order = sorted(range(F), key=lambda f: (given[f"tbl_{f}"].shape[0], f))
    numbers = np.zeros((128, 2 + HOT_DEEP), np.float32)
    numbers[:, 0] = -(np.arange(128) * HOT_DEEP + (HOT_DEEP - 1) / 2)
    numbers[:, 1] = np.arange(128) * HOT_DEEP
    numbers[:, 2:] = np.arange(HOT_DEEP)
    source = np.zeros((128, SOURCES), np.int64) - 1
    for i in range(SOURCES):
        for row, field in fields_of(i):
            source[row, i] = field
    w0 = np.concatenate([given["L0_rec_W0"].reshape(H, F * F), np.zeros((H, 1), np.float32)], axis=1)
    ab, ba = np.full((128, NP), F * F), np.full((128, NP), F * F)
    for k, (i, j) in enumerate(PAIRS):
        for row in range(128):
            a, b = source[row, i], source[row, j]
            if a >= 0 and b >= 0:
                ab[row, k] = order[a] * F + order[b]
                if a != b:
                    ba[row, k] = order[b] * F + order[a]
    select = np.zeros((PARTS, F, SOURCES, 128), np.float32)
    for i in range(SOURCES):
        for row, field in fields_of(i):
            select[:, field, i, row] = 1
    own = np.zeros((128, GB), np.float32)
    own[np.arange(128), np.arange(128) // D % GB] = 1
    ids = given["ids"][:, order].reshape(TILES, CHUNKS, 2, GROUPS, GB, F).transpose(0, 1, 3, 2, 4, 5)
    return {
        "ids": ids.reshape(BATCH, F),
        "hot_ids_given": np.concatenate([ids.reshape(BATCH, F)[:BT, :LOT[0]].T,
                                         ids.reshape(BATCH, F)[BT:2 * BT, :HOT_NEXT].T]),
        "hot_numbers": numbers,
        **{f"tbl_{n}": given[f"tbl_{f}"] for n, f in enumerate(order)},
        "ctx_t": given["dense_ctx"].T,
        "w0_ab": w0.T[ab],
        "w0_ba": w0.T[ba],
        "w1": given["L0_rec_W1"].reshape(H, F, H)[:, order].transpose(2, 1, 0),
        "select": select.reshape(PARTS * F, SOURCES, 128),
        "select_t": np.tile(np.eye(F, dtype=np.float32), (PARTS, 1)),
        "own": own,
        "ident": np.eye(128, dtype=np.float32),
        "w_top1z": given["W_top1"][:2 * H].reshape(2, H, M1).transpose(1, 0, 2),
        "w_top1c": given["W_top1"][2 * H:],
        "b_top1": given["b_top1"].reshape(M1 // 128, 128).T,
        "w_top2": given["W_top2"].reshape(M1 // 128, 128, M2).transpose(1, 0, 2),
        "b_top2": given["b_top2"].reshape(M2 // 128, 128).T,
        "w_top3": given["W_top3"].reshape(M2 // 128, 128).T,
    }


def kernel(**inputs):
    import concourse.bacc as bacc
    from concourse.bass_utils import run_bass_kernel_spmd

    nc = bacc.Bacc("TRN2", target_bir_lowering=False, num_devices=1)
    arrays = {n: np.ascontiguousarray(a) for n, a in layouts({n: np.asarray(a) for n, a in inputs.items()}).items()}
    args = {n: nc.dram_tensor(n, a.shape, mybir.dt.from_np(a.dtype), kind="ExternalInput").ap()
            for n, a in arrays.items()}
    tables = [args.pop(f"tbl_{f}") for f in range(F)]
    out = nc.dram_tensor("out", (BATCH, 1), mybir.dt.float32, kind="ExternalOutput").ap()
    build(nc, tables=tables, out=out, **args)
    r = run_bass_kernel_spmd(nc, [arrays], core_ids=[0])
    return r.results[0]["out"]
```
